# Optimizing a Trainium2 kernel written in Bass

```python
import numpy as np
import jax
import jax.numpy as jnp

def _softmax(x, axis=-1):
    return jax.nn.softmax(x, axis=axis)

def _gelu(x):
    return jax.nn.gelu(x, approximate=True)

def _silu(x):
    return jax.nn.silu(x)

def _sigmoid(x):
    return jax.nn.sigmoid(x)

def _layernorm(x, axis=-1, eps=1e-05):
    m = jnp.mean(x, axis=axis, keepdims=True)
    v = jnp.var(x, axis=axis, keepdims=True)
    return (x - m) / jnp.sqrt(v + eps)

def _scatter_add(tgt, idx, src, axis=0):
    return tgt.at[idx].add(src)

def _segment_sum(src, seg, n):
    return jax.ops.segment_sum(src, seg, n)
kernel_name = 'mk_recurrent_d1_jaxref_r4_5720d6'

def setup_inputs(seed: int=0):
    np.random.seed(seed)
    _w = jnp.asarray

    def _L0_attn_setup():
        import jax, jax.numpy as jnp
        import numpy as np
        D_MODEL = 256
        D_STATE = 16
        LN_EPS = 1e-05

        def _layernorm(x, w, b):
            mu = jnp.mean(x, axis=-1, keepdims=True)
            var = jnp.mean(jnp.square(x - mu), axis=-1, keepdims=True)
            return (x - mu) * jax.lax.rsqrt(var + LN_EPS) * w + b
        key = jax.random.key(seed)
        ks = jax.random.split(key, 12)
        B, S, D, N = (8, 1024, D_MODEL, D_STATE)
        sD = 1.0 / np.sqrt(D)
        sN = 1.0 / np.sqrt(N)
        return {'x': jax.random.normal(ks[0], (B, S, D), dtype=jnp.float32), 'Ws': jax.random.uniform(ks[1], (N, D), jnp.float32, -sD, sD), 'bs': jax.random.uniform(ks[2], (N,), jnp.float32, -sD, sD), 'Wi': jax.random.uniform(ks[3], (N, D), jnp.float32, -sD, sD), 'bi': jax.random.uniform(ks[4], (N,), jnp.float32, -sD, sD), 'Wo': jax.random.uniform(ks[5], (D, N), jnp.float32, -sN, sN), 'bo': jax.random.uniform(ks[6], (D,), jnp.float32, -sN, sN), 'Wg': jax.random.uniform(ks[7], (D, D), jnp.float32, -sD, sD), 'bg': jax.random.uniform(ks[8], (D,), jnp.float32, -sD, sD), 'ln_w': jnp.ones((D,), jnp.float32), 'ln_b': jnp.zeros((D,), jnp.float32), 'A': jax.random.normal(ks[9], (N, N), dtype=jnp.float32) * 0.01}
    _L0_attn_in = _L0_attn_setup()

    def _L0_ffn_setup():
        import jax, jax.numpy as jnp
        import numpy as np
        from jax import lax
        DIM = 256
        INTER = 128
        N_EXPERTS = 16
        TOPK = 4
        ROUTE_SCALE = 2.5
        VOCAB = 8000

        def _silu_and_mul(gu):
            gate, up = jnp.split(gu, 2, axis=-1)
            return jax.nn.silu(gate) * up
        key = jax.random.key(seed)
        ks = jax.random.split(key, 8)
        x = jax.random.normal(ks[0], (2, 128, DIM), dtype=jnp.float32)
        input_ids = jax.random.randint(ks[1], (2, 128), 0, VOCAB)
        s = 0.02
        gate_w = jax.random.normal(ks[2], (N_EXPERTS, DIM), dtype=jnp.float32) * s
        gate_b = jax.random.normal(ks[3], (N_EXPERTS,), dtype=jnp.float32) * s
        w13 = jax.random.normal(ks[4], (N_EXPERTS, 2 * INTER, DIM), dtype=jnp.float32) * s
        w2 = jax.random.normal(ks[5], (N_EXPERTS, DIM, INTER), dtype=jnp.float32) * s
        w13_s = jax.random.normal(ks[6], (2 * INTER, DIM), dtype=jnp.float32) * s
        w2_s = jax.random.normal(ks[7], (DIM, INTER), dtype=jnp.float32) * s
        return {'x': x, 'input_ids': input_ids, 'gate_w': gate_w, 'gate_b': gate_b, 'w13': w13, 'w2': w2, 'w13_s': w13_s, 'w2_s': w2_s}
    _L0_ffn_in = _L0_ffn_setup()
    _d = {'L0_attn_x': _L0_attn_in['x'], 'L0_attn_Ws': _L0_attn_in['Ws'], 'L0_attn_bs': _L0_attn_in['bs'], 'L0_attn_Wi': _L0_attn_in['Wi'], 'L0_attn_bi': _L0_attn_in['bi'], 'L0_attn_Wo': _L0_attn_in['Wo'], 'L0_attn_bo': _L0_attn_in['bo'], 'L0_attn_Wg': _L0_attn_in['Wg'], 'L0_attn_bg': _L0_attn_in['bg'], 'L0_attn_ln_w': _L0_attn_in['ln_w'], 'L0_attn_ln_b': _L0_attn_in['ln_b'], 'L0_attn_A': _L0_attn_in['A'], 'L0_ffn_input_ids': _L0_ffn_in['input_ids'], 'L0_ffn_gate_w': _L0_ffn_in['gate_w'], 'L0_ffn_gate_b': _L0_ffn_in['gate_b'], 'L0_ffn_w13': _L0_ffn_in['w13'], 'L0_ffn_w2': _L0_ffn_in['w2'], 'L0_ffn_w13_s': _L0_ffn_in['w13_s'], 'L0_ffn_w2_s': _L0_ffn_in['w2_s']}
    _x0 = _d['L0_attn_x']
    _d['L0_attn_x'] = jax.random.normal(jax.random.fold_in(jax.random.key(seed), 1), (2, 2048, 256), dtype=_x0.dtype)
    del _x0
    return _d

def reference(L0_attn_x, L0_attn_Ws, L0_attn_bs, L0_attn_Wi, L0_attn_bi, L0_attn_Wo, L0_attn_bo, L0_attn_Wg, L0_attn_bg, L0_attn_ln_w, L0_attn_ln_b, L0_attn_A, L0_ffn_input_ids, L0_ffn_gate_w, L0_ffn_gate_b, L0_ffn_w13, L0_ffn_w2, L0_ffn_w13_s, L0_ffn_w2_s):

    def _L0_attn_ref(x, Ws, bs, Wi, bi, Wo, bo, Wg, bg, ln_w, ln_b, A):
        import jax, jax.numpy as jnp
        import numpy as np
        D_MODEL = 256
        D_STATE = 16
        LN_EPS = 1e-05

        def _layernorm(x, w, b):
            mu = jnp.mean(x, axis=-1, keepdims=True)
            var = jnp.mean(jnp.square(x - mu), axis=-1, keepdims=True)
            return (x - mu) * jax.lax.rsqrt(var + LN_EPS) * w + b
        B, S, D = x.shape
        residual = x
        xn = _layernorm(x, ln_w, ln_b)
        u = jnp.einsum('bsd,nd->bsn', xn, Ws) + bs + jnp.einsum('bsd,nd->bsn', xn, Wi) + bi
        h0 = jnp.zeros((B, A.shape[0]), x.dtype)

        def step(h, u_t):
            h = jnp.tanh(h @ A.T + u_t)
            return (h, h)
        _, H = jax.lax.scan(step, h0, jnp.swapaxes(u, 0, 1))
        H = jnp.swapaxes(H, 0, 1)
        out = jnp.einsum('bsn,dn->bsd', H, Wo) + bo
        gate = jax.nn.sigmoid(jnp.einsum('bsd,ed->bse', xn, Wg) + bg)
        return out * gate + residual

    def _L0_ffn_ref(x, input_ids, gate_w, gate_b, w13, w2, w13_s, w2_s):
        import jax, jax.numpy as jnp
        import numpy as np
        from jax import lax
        DIM = 256
        INTER = 128
        N_EXPERTS = 16
        TOPK = 4
        ROUTE_SCALE = 2.5
        VOCAB = 8000

        def _silu_and_mul(gu):
            gate, up = jnp.split(gu, 2, axis=-1)
            return jax.nn.silu(gate) * up
        B, S, D = x.shape
        xt = x.reshape(-1, D)
        T = xt.shape[0]
        scores = jax.nn.sigmoid(xt.astype(jnp.float32) @ gate_w.T)
        biased = scores + gate_b
        _, idx = lax.top_k(biased, TOPK)
        w = jnp.take_along_axis(scores, idx, axis=-1)
        w = w / jnp.sum(w, axis=-1, keepdims=True)
        w = w * ROUTE_SCALE
        comb = jnp.zeros((T, N_EXPERTS), jnp.float32)
        comb = comb.at[jnp.arange(T)[:, None], idx].add(w)
        comb = comb.astype(x.dtype)

        def expert_body(y, args):
            w13_e, w2_e, c_e = args
            h = _silu_and_mul(xt @ w13_e.T)
            return (y + c_e[:, None] * (h @ w2_e.T), None)
        y, _ = lax.scan(expert_body, jnp.zeros_like(xt), (w13, w2, comb.T))
        y = y + _silu_and_mul(xt @ w13_s.T) @ w2_s.T
        return y.astype(x.dtype).reshape(B, S, D)
    x = L0_attn_x
    xn = _layernorm(x, axis=-1)
    s = _L0_attn_ref(xn, L0_attn_Ws, L0_attn_bs, L0_attn_Wi, L0_attn_bi, L0_attn_Wo, L0_attn_bo, L0_attn_Wg, L0_attn_bg, L0_attn_ln_w, L0_attn_ln_b, L0_attn_A)
    g = _silu(_L0_ffn_ref(xn, L0_ffn_input_ids, L0_ffn_gate_w, L0_ffn_gate_b, L0_ffn_w13, L0_ffn_w2, L0_ffn_w13_s, L0_ffn_w2_s))
    x = x + s * g
    return x

_drawn_inputs = setup_inputs


def setup_inputs(seed=0):
    import zlib

    import numpy as np

    out = dict(_drawn_inputs(seed))
    spreads = {'L0_attn_ln_w': (1.0, 0.6), 'L0_attn_ln_b': (0.0, 0.8)}
    factors = {'L0_attn_Ws': 8.0,
     'L0_attn_bs': 8.0,
     'L0_attn_Wi': 8.0,
     'L0_attn_bi': 8.0,
     'L0_attn_Wo': 8.0,
     'L0_attn_bo': 8.0,
     'L0_attn_Wg': 8.0,
     'L0_attn_bg': 8.0,
     'L0_attn_A': 8.0,
     'L0_ffn_gate_w': 8.0,
     'L0_ffn_gate_b': 8.0,
     'L0_ffn_w13': 7.447,
     'L0_ffn_w2': 7.402,
     'L0_ffn_w13_s': 8.0,
     'L0_ffn_w2_s': 8.0}
    for name, (base, spread) in spreads.items():
        noise = np.random.default_rng([zlib.crc32(name.encode()), seed]).standard_normal(out[name].shape)
        drawn = base * np.exp(spread * noise) if base else spread * noise
        out[name] = jnp.asarray(drawn.astype(out[name].dtype))
    for name, factor in factors.items():
        out[name] = (out[name] * factor).astype(out[name].dtype)
    return out
```

```python
import concourse.bass as bass
from concourse import mybir
from contextlib import ExitStack

import numpy as np


class Counter:

    def __init__(self, handle, unit=1):
        self.handle, self.unit, self.value = handle, unit, 0

    def give(self):
        self.value += self.unit
        return self, self.value


class Queue:

    def __init__(self, counter):
        self.steps, self.counter = [], counter

    def do(self, make, *marks, counter=None, quiet=False):
        mark = None if quiet else (counter or self.counter).give()
        self.steps.append((make, marks, mark))
        return mark

    def emit(self, engine):
        reached = {}
        for make, marks, mark in self.steps:
            for sig, value in marks:
                if reached.get(sig.handle.name, 0) < value:
                    engine.wait_ge(sig.handle, value)
                    reached[sig.handle.name] = value
            instruction = make(engine)
            if mark is not None:
                instruction.then_inc(mark[0].handle, mark[0].unit)


def recurrent_gated_moe(nc: bass.Bass, x, w13t, w2t, router_wt, router_b, gate_wt, gate_b_row, state_wt, input_wt,
                        state_b, input_b, rec_at, out_wt, out_b_row, ln_w, ln_b, out):
    f32, f16, bf16, i32, u32 = (mybir.dt.float32, mybir.dt.float16, mybir.dt.bfloat16, mybir.dt.int32,
                                mybir.dt.uint32)
    ALU, ACT, AX = mybir.AluOpType, mybir.ActivationFunctionType, mybir.AxisListType

    P = 128
    T, D = x.shape
    KD = D // P
    NT = T // P
    E = router_wt.shape[2]
    NE = w13t.shape[1]
    N = rec_at.shape[0]
    F = w2t.shape[0]
    TOPK = 4
    ROUTE_SCALE = 2.5
    EPS = 1e-5
    BT = 4
    NB = NT // BT
    BW = BT * P
    G = P // N
    L = 16
    C = BW // L
    SEQS = 2
    XS, WS = 16.0, 64.0
    DESCALE = 1.0 / (XS * WS)

    ctx = ExitStack()
    with ctx:
        def sb(name, shape, dt=f32):
            return ctx.enter_context(nc.sbuf_tensor(name, shape, dt))

        def pb(name, shape, dt=f32):
            return ctx.enter_context(nc.psum_tensor(name, shape, dt))

        def sem(name, unit=1):
            return Counter(ctx.enter_context(nc.semaphore(name)), unit)

        x_sb = sb("x_sb", [P, NT, D])
        xn_f = sb("xn_f", [P, BT, D])
        mix_sb = sb("mix_sb", [P, NT, D])
        y_sb = sb("y_sb", [P, NT, D])
        xT = sb("xT", [P, 2, KD, T], f16)
        xn_parts = sb("xn_parts", [P, 2, BT, D], f16)
        zn_f = sb("zn_f", [P, BT, D])
        zn_parts = sb("zn_parts", [P, 2, BT, D], f16)
        zT = sb("zT", [P, 2, KD, BW], f16)
        stats = sb("stats", [P, NT, 6])
        mean_var = sb("mean_var", [P, NT, 2])
        var2 = sb("var2", [P, 2, NT])
        root2 = sb("root2", [P, 2, NT])
        newton = sb("newton", [P, 2, NT])
        rstd2 = sb("rstd2", [P, 2, NT])
        ident_f = sb("ident_f", [P, P])
        ident_h = sb("ident_h", [P, P], f16)
        shift_f = sb("shift_f", [P, P])
        ones_col = sb("ones_col", [P, 1])
        ones_row3 = sb("ones_row3", [3, P], bf16)
        lnw_sb = sb("lnw_sb", [P, KD])
        lnb_sb = sb("lnb_sb", [P, KD])
        router_f = sb("router_f", [P, KD, E])
        router_p = sb("router_p", [P, 2, KD, E], f16)
        router_bias = sb("router_bias", [P, E])
        gate_f = sb("gate_f", [P, KD, D])
        gate_p = sb("gate_p", [P, 2, KD, D], f16)
        state_f = sb("state_f", [P, 2, KD, N])
        state_sum = sb("state_sum", [P, KD, N])
        state_rep = sb("state_rep", [P, KD, G, N])
        state_w = sb("state_w", [P, KD, N])
        state_pad = sb("state_pad", [P, 2, KD, 2 * P - N], f16)
        sbias = sb("sbias", [P, 2])
        state_bias = sb("state_bias", [P, 1])
        rec_bd = sb("rec_bd", [P, P])
        outw_p = sb("outw_p", [P, 2, G, D], f16)
        bias_rows = sb("bias_rows", [3, 2, D], bf16)
        scores = sb("scores", [P, NT, E])
        iota_e = sb("iota_e", [P, E])
        comb = sb("comb", [P, NT, E])
        norm = sb("norm", [P, NT])
        w_stage = sb("w_stage", [P, 2, KD * 2 * F + D])
        w_part = sb("w_part", [P, 2, 2, KD * 2 * F + D], f16)
        silu_f = zn_f[:, :, :].rearrange("p (s b) d -> p s (b d)", s=2)
        h_f = zn_parts[:, :, :, :].bitcast(f32).rearrange("p s b d -> p s (b d)")
        h_p = xn_parts[:, :, :, :].rearrange("p s (i b) d -> p s i (b d)", i=2)
        u_sb = sb("u_sb", [P, C, L])
        H = [sb(f"H{i}", [P, C, L]) for i in range(2)]
        H_p = sb("H_p", [P, 2, C, L], f16)
        start = [sb(f"start{i}", [P, C]) for i in range(2)]
        differ = sb("differ", [P, C])
        differ_max = sb("differ_max", [P, 1])
        flag = sb("flag", [1, 1], i32)

        bank = [pb(f"bank{i}", [P, 512]) for i in range(8)]

        scratch, at = y_sb[:, :, :].rearrange("p n d -> p (n d)"), [0]

        def part_of_y(width, pattern=None, dt=f32, rows=P, **dims):
            v = scratch[0:rows, at[0]:at[0] + width]
            at[0] += width
            v = v if dt is f32 else v.bitcast(dt)
            return v.rearrange(pattern, **dims) if pattern else v

        bias_in = part_of_y(2 * D, "p (b d) -> p b d", rows=1, b=2)
        bias_f = part_of_y(2 * D, "p (b d) -> p b d", rows=1, b=2)
        bias_part = part_of_y(3 * D, "p (j b d) -> p j b d", dt=bf16, rows=1, j=3, b=2)
        outw_f = part_of_y(D)
        outw_c = part_of_y(D, "p (i d) -> p i d", dt=f16, i=2)
        biased = part_of_y(NT * E, "p (n e) -> p n e", e=E)
        top8 = part_of_y(NT * 8, "p (n e) -> p n e", e=8)
        idx8 = part_of_y(NT * 8, "p (n e) -> p n e", dt=u32, e=8)
        idx_f = part_of_y(NT * TOPK, "p (n e) -> p n e", e=TOPK)
        onehot = part_of_y(NT * E, "p (n e) -> p n e", e=E)

        s_pe, s_act, s_dve, s_pool = sem("pe_done"), sem("act_done"), sem("dve_done"), sem("pool_done")
        pe, act, dve, pool, sync = Queue(s_pe), Queue(s_act), Queue(s_dve), Queue(s_pool), Queue(None)

        def load(dst, src, name, *marks, queue=None):
            return (queue or sync).do(lambda e: e.dma_start(dst, src), *marks, counter=sem(name, 16))

        XL = 4
        x_view = x.rearrange("(n p) d -> p n d", p=P)
        x_in = [load(x_sb[:, n:n + XL, :], x_view[:, n:n + XL, :], f"x_in{n}") for n in range(0, NT, XL)]
        lnw_in = load(lnw_sb[:, :], ln_w, "lnw_in", queue=act)
        lnb_in = load(lnb_sb[:, :], ln_b, "lnb_in", queue=act)
        router_in = load(router_f[:, :, :], router_wt, "router_in", queue=act)
        gate_in = load(gate_f[:, :, :], gate_wt, "gate_in", queue=act)
        state_in = load(state_f[:, 0, :, :], state_wt, "state_in", queue=act)
        input_in = load(state_f[:, 1, :, :], input_wt, "input_in", queue=act)
        sb_in = load(sbias[:, 0:1], state_b, "sb_in", queue=act)
        ib_in = load(sbias[:, 1:2], input_b, "ib_in", queue=act)
        gb_in = load(bias_in[:, 0, :], gate_b_row, "gb_in", queue=act)
        ob_in = load(bias_in[:, 1, :], out_b_row, "ob_in", queue=act)
        rb_in = load(router_bias[:, :], router_b.broadcast_to([P, E]), "rb_in", queue=act)

        z = [pool.do(lambda e, t=t: e.memset(t, 0.0)) for t in
             (ident_f[:, :], ident_h[:, :], shift_f[:, :], rec_bd[:, :], outw_p[:, :, :, :], state_pad[:, :, :, :])]
        idf = pool.do(lambda e: e.affine_select(out=ident_f[:, :], in_=ident_f[:, :], compare_op=ALU.not_equal, fill=1.0,
                                                base=0, pattern=[[-1, P]], channel_multiplier=1), z[0])
        idh = pool.do(lambda e: e.affine_select(out=ident_h[:, :], in_=ident_h[:, :], compare_op=ALU.not_equal, fill=1.0,
                                                base=0, pattern=[[-1, P]], channel_multiplier=1), z[1])
        sh0 = pool.do(lambda e: e.affine_select(out=shift_f[:, :], in_=shift_f[:, :], compare_op=ALU.not_equal,
                                                fill=1.0, base=N, pattern=[[-1, P]], channel_multiplier=1), z[2])
        shift_ready = pool.do(lambda e: e.memset(shift_f[:, P // SEQS:P // SEQS + N], 0.0), sh0)
        ones_ready = [pool.do(lambda e: e.memset(ones_col[:, :], 1.0)), pool.do(lambda e: e.memset(ones_row3[:, :], 1.0))]
        iota_ready = pool.do(lambda e: e.iota(iota_e[:, :], pattern=[[1, E]], base=0, channel_multiplier=0,
                                              allow_small_or_imprecise_dtypes=True))
        s_bd, s_ow = sem("rec_in", 16), sem("outw_placed", 16)
        for g in range(G):
            rec_in = sync.do(lambda e, g=g: e.dma_start(rec_bd[g * N:(g + 1) * N, g * N:(g + 1) * N], rec_at), z[3],
                             counter=s_bd)
        outw_in = load(outw_f[:, :], out_wt, "outw_in", queue=act)

        WG = KD * 2 * F
        w_in, w_ready, w_used = {}, {}, {}

        def split_weights(e):
            free = w_used[e - 2] if e >= 2 else ()
            hi = act.do(lambda q: q.activation(w_part[:, e % 2, 0, :], w_stage[:, e % 2, :], ACT.Copy, scale=WS),
                        *w_in[e], *free)
            lo = dve.do(lambda q: q.scalar_tensor_tensor(out=w_part[:, e % 2, 1, :], in0=w_stage[:, e % 2, :], scalar=WS,
                                                         in1=w_part[:, e % 2, 0, :], op0=ALU.mult, op1=ALU.subtract), hi)
            w_ready[e] = (hi, lo)

        ORDER = [NE - 1] + list(range(NE - 1))

        r_hi = dve.do(lambda e: e.tensor_scalar(router_p[:, 0, :, :], router_f[:, :, :], WS, None, ALU.mult), router_in)
        r_lo = dve.do(lambda e: e.scalar_tensor_tensor(out=router_p[:, 1, :, :], in0=router_f[:, :, :], scalar=WS,
                                                       in1=router_p[:, 0, :, :], op0=ALU.mult, op1=ALU.subtract), r_hi)
        ssum = dve.do(lambda e: e.tensor_tensor(state_sum[:, :, :], state_f[:, 0, :, :], state_f[:, 1, :, :], ALU.add),
                      state_in, input_in)
        srep = dve.do(lambda e: e.tensor_copy(state_rep[:, :, :, :],
                                              state_sum[:, :, None, :].to_broadcast([P, KD, G, N])), ssum)
        MID = P - N
        for k in range(KD):
            sw = dve.do(lambda e, k=k: e.tensor_scalar(state_w[:, k, :], state_sum[:, k, :], lnw_sb[:, k:k + 1], WS,
                                                       ALU.mult, ALU.mult), ssum, lnw_in)
        sp_hi = dve.do(lambda e: e.tensor_copy(state_pad[:, 0, :, MID:P], state_w[:, :, :]), sw, z[5])
        sp_lo = dve.do(lambda e: e.tensor_tensor(state_pad[:, 1, :, MID:P], state_w[:, :, :], state_pad[:, 0, :, MID:P],
                                                 ALU.subtract), sp_hi)
        for k in range(KD):
            sb_mm = pe.do(lambda e, k=k: e.matmul(bank[7][:, 0:1], state_rep[:, k, :, :].rearrange("p g n -> p (g n)"),
                                                  lnb_sb[:, k:k + 1], start=k == 0, stop=k == KD - 1), srep, lnb_in)
        sb1 = dve.do(lambda e: e.tensor_tensor(state_bias[:, :], sbias[:, 0:1], sbias[:, 1:2], ALU.add), sb_in, ib_in)
        state_bias_ready = dve.do(lambda e: e.tensor_tensor(state_bias[:, :], state_bias[:, :], bank[7][:, 0:1], ALU.add),
                                  sb1, sb_mm)
        for k in range(KD):
            gb_mm = pe.do(lambda e, k=k: e.matmul(bank[6][0:1, 0:D], lnb_sb[:, k:k + 1], gate_f[:, k, :], start=k == 0,
                                                  stop=k == KD - 1), gate_in, lnb_in)
        b0 = dve.do(lambda e: e.tensor_tensor(bias_f[:, 0, :], bias_in[:, 0, :], bank[6][0:1, 0:D], ALU.add), gb_in, gb_mm)
        b1 = dve.do(lambda e: e.tensor_scalar(bias_f[:, 0, :], bias_f[:, 0, :], 1.0 / DESCALE, None, ALU.mult), b0)
        b2 = dve.do(lambda e: e.tensor_scalar(bias_f[:, 1, :], bias_in[:, 1, :], 1.0 / DESCALE, None, ALU.mult), ob_in)
        last = b2
        for j in range(3):
            last = dve.do(lambda e, j=j: e.tensor_copy(bias_part[:, j, :, :], bias_f[:, :, :]), b1, last)
            part = last
            if j < 2:
                last = dve.do(lambda e, j=j: e.tensor_tensor(bias_f[:, :, :], bias_f[:, :, :], bias_part[:, j, :, :],
                                                             ALU.subtract), last)
        s_br = sem("bias_rows_in", 16)
        for j in range(3):
            bias_ready = sync.do(lambda e, j=j: e.dma_start(bias_rows[j:j + 1, :, :], bias_part[:, j, :, :]), part,
                                 counter=s_br)
        for k in range(KD):
            gw = dve.do(lambda e, k=k: e.tensor_scalar(gate_f[:, k, :], gate_f[:, k, :], lnw_sb[:, k:k + 1], WS, ALU.mult,
                                                       ALU.mult), gb_mm, lnw_in)
        g_hi = dve.do(lambda e: e.tensor_copy(gate_p[:, 0, :, :], gate_f[:, :, :]), gw)
        g_lo = dve.do(lambda e: e.tensor_tensor(gate_p[:, 1, :, :], gate_f[:, :, :], gate_p[:, 0, :, :], ALU.subtract), g_hi)
        ow_hi = dve.do(lambda e: e.tensor_scalar(outw_c[:, 0, :], outw_f[:, :], WS, None, ALU.mult), outw_in)
        ow_lo = dve.do(lambda e: e.scalar_tensor_tensor(out=outw_c[:, 1, :], in0=outw_f[:, :], scalar=WS,
                                                        in1=outw_c[:, 0, :], op0=ALU.mult, op1=ALU.subtract), ow_hi)
        for g in range(G):
            outw_ready = sync.do(lambda e, g=g: e.dma_start(outw_p[g * N:(g + 1) * N, :, g, :],
                                                            outw_c[g * N:(g + 1) * N, :, :]), ow_lo, z[4], counter=s_ow)

        SB = NT // 4
        rstd_ready = []

        def norm_stats(q):
            r = slice(q * SB, (q + 1) * SB)
            for n in range(q * SB, (q + 1) * SB):
                st = dve.do(lambda e, n=n: e.bn_stats(stats[:, n, :], x_sb[:, n, :]), x_in[n // XL])
                mv = dve.do(lambda e, n=n: e.bn_aggr(mean_var[:, n, :], stats[:, n, :]), st)
            v = mean_var[:, r, 1]
            a = dve.do(lambda e: e.tensor_scalar(var2[:, 0, r], v, 1.0, EPS, ALU.mult, ALU.add), mv)
            b = dve.do(lambda e: e.tensor_scalar(var2[:, 1, r], v, 1.0 + EPS, EPS * EPS, ALU.mult, ALU.add), mv)
            s = act.do(lambda e: e.activation(root2[:, :, r], var2[:, :, r], ACT.Sqrt), a, b)
            y = dve.do(lambda e: e.reciprocal(rstd2[:, :, r], root2[:, :, r]), s)
            y = dve.do(lambda e: e.tensor_tensor(newton[:, :, r], rstd2[:, :, r], rstd2[:, :, r], ALU.mult), y)
            y = dve.do(lambda e: e.tensor_tensor(newton[:, :, r], newton[:, :, r], var2[:, :, r], ALU.mult), y)
            y = dve.do(lambda e: e.tensor_scalar(newton[:, :, r], newton[:, :, r], -0.5 * XS, 1.5 * XS, ALU.mult, ALU.add), y)
            rstd_ready.append(dve.do(lambda e: e.tensor_tensor(rstd2[:, :, r], rstd2[:, :, r], newton[:, :, r], ALU.mult), y))

        TP = [bank[0], bank[1]]
        ROUTE, U = bank[2], bank[3]
        GATE = [bank[4], bank[5]]
        bank_free = {0: None, 1: None}
        parts_free, zf_free, zT_free = (), (), {}
        xT_ready, gate_ready, tp = {}, {}, 0
        gate_bank_free = {0: (b0,), 1: ()}
        sqrt_last = None
        for q in range(4):
            norm_stats(q)
        for b in range(NB):
            ready = rstd_ready[b * BT // SB]
            for n in range(b * BT, (b + 1) * BT):
                nx = dve.do(lambda e, n=n, i=n % BT: e.tensor_scalar(xn_f[:, i, :], x_sb[:, n, :], mean_var[:, n, 0:1],
                                                           rstd2[:, 0, n:n + 1], ALU.subtract, ALU.mult),
                            ready, *zf_free)
            for n in range(b * BT, (b + 1) * BT):
                nz = dve.do(lambda e, n=n, i=n % BT: e.tensor_scalar(zn_f[:, i, :], x_sb[:, n, :], mean_var[:, n, 0:1],
                                                                     rstd2[:, 1, n:n + 1], ALU.subtract, ALU.mult),
                            ready, *zf_free)
            xh = act.do(lambda e: e.activation(xn_parts[:, 0, :, :], xn_f[:, :, :], ACT.Copy), nx, *parts_free)
            xl = pool.do(lambda e: e.tensor_tensor(xn_parts[:, 1, :, :], xn_f[:, :, :], xn_parts[:, 0, :, :],
                                                   ALU.subtract), xh)
            zh = act.do(lambda e: e.activation(zn_parts[:, 0, :, :], zn_f[:, :, :], ACT.Copy), nz)
            zl = pool.do(lambda e: e.tensor_tensor(zn_parts[:, 1, :, :], zn_f[:, :, :], zn_parts[:, 0, :, :],
                                                   ALU.subtract), zh)
            zf_free = (zl,)
            made = []
            for src, dst, hi, lo, cols in ((xn_parts, xT, xh, xl, b * BW), (zn_parts, zT, zh, zl, 0)):
                for part in range(2):
                    tb = TP[tp % 2].bitcast(f16) if False else TP[tp % 2][:, :].bitcast(f16)
                    free = bank_free[tp % 2]
                    for k in range(KD):
                        for i in range(BT):
                            t = pe.do(lambda e, k=k, i=i, part=part, tb=tb, src=src:
                                      e.transpose(tb[:, (k * BT + i) * P:(k * BT + i + 1) * P],
                                                  src[:, part, i, k * P:(k + 1) * P], ident_h[:, :]),
                                      idh, lo if part else hi, *((free,) if free else ()))
                    extra = zT_free.get(b - 1, ()) if src is zn_parts else ()
                    eng = act if part == 0 else dve
                    view = tb.rearrange("p (k t) -> p k t", k=KD)
                    d = dst[:, part, :, cols:cols + BW]
                    if eng is act:
                        ev = act.do(lambda e, d=d, view=view: e.activation(d, view, ACT.Copy), t, *extra)
                    else:
                        ev = dve.do(lambda e, d=d, view=view: e.tensor_copy(d, view), t, *extra)
                    bank_free[tp % 2] = ev
                    made.append(ev)
                    tp += 1
            parts_free = (t,)
            xT_ready[b] = made[0:2]
            for i in range(BT):
                n = b * BT + i
                for j, (pa, pw, k) in enumerate([(pa, pw, k) for k in range(KD) for pa in range(2) for pw in range(2)]):
                    rt = pe.do(lambda e, n=n, j=j, pa=pa, pw=pw, k=k:
                               e.matmul(ROUTE[:, n * E:(n + 1) * E], xT[:, pa, k, n * P:(n + 1) * P],
                                        router_p[:, pw, k, :], start=j == 0, stop=j == 2 * 2 * KD - 1), *made[0:2], r_lo)
            for k in range(KD):
                for j, (pz, pw) in enumerate(((0, 0), (0, 1), (1, 0))):
                    um = pe.do(lambda e, b=b, k=k, j=j, pz=pz, pw=pw:
                               e.matmul(U[:, :], state_pad[:, pw, k, MID - b * N:MID - b * N + P], zT[:, pz, k, :],
                                        start=b == 0 and k == 0 and j == 0, stop=b == NB - 1 and k == KD - 1 and j == 2),
                               *made[2:4], sp_lo)
            for i in range(BT):
                n = b * BT + i
                gbk = GATE[n % 2]
                for k in range(KD):
                    for pz, pw in ((0, 0), (0, 1), (1, 0)):
                        pe.do(lambda e, i=i, k=k, pz=pz, pw=pw, gbk=gbk:
                              e.matmul(gbk[:, 0:D], zT[:, pz, k, i * P:(i + 1) * P], gate_p[:, pw, k, :],
                                       start=k == 0 and pz == 0 and pw == 0, stop=False),
                              g_lo, *gate_bank_free[n % 2], quiet=True)
                gm = pe.do(lambda e, gbk=gbk: e.matmul(gbk[:, 0:D], ones_row3[:, :], bias_rows[:, 0, :], start=False,
                                                       stop=True), bias_ready, ones_ready[1])
                gs = act.do(lambda e, n=n, gbk=gbk: e.activation(mix_sb[:, n, :], gbk[:, 0:D], ACT.Sigmoid,
                                                                 scale=DESCALE), gm)
                gate_bank_free[n % 2] = (gs,)
                gate_ready[n] = gs
            zT_free[b] = (gm,)

        u_ready = act.do(lambda e: e.activation(u_sb[:, :, :].rearrange("p c j -> p (c j)"), U[:, :], ACT.Identity,
                                                bias=state_bias[:, 0:1], scale=DESCALE), um, state_bias_ready)

        sc = act.do(lambda e: e.activation(scores[:, :, :].rearrange("p n e -> p (n e)"), ROUTE[:, :], ACT.Sigmoid,
                                           scale=DESCALE), rt)
        bi = dve.do(lambda e: e.tensor_tensor(biased[:, :, :], scores[:, :, :],
                                              router_bias[:, None, :].to_broadcast([P, NT, E]), ALU.add), sc, rb_in)
        for n in range(NT):
            mx = dve.do(lambda e, n=n: e.max(top8[:, n, :], biased[:, n, :]), bi)
            ix = dve.do(lambda e, n=n: e.max_index(idx8[:, n, :], top8[:, n, :], biased[:, n, :]), mx)
        xf = dve.do(lambda e: e.tensor_copy(idx_f[:, :, :], idx8[:, :, 0:TOPK]), ix)
        m = xf
        for k in range(TOPK):
            dst = comb[:, :, :] if k == 0 else onehot[:, :, :]
            m = dve.do(lambda e, k=k, dst=dst: e.tensor_tensor(dst, idx_f[:, :, k:k + 1].to_broadcast([P, NT, E]),
                                                               iota_e[:, None, :].to_broadcast([P, NT, E]),
                                                               ALU.is_equal), m, iota_ready)
            if k:
                m = dve.do(lambda e: e.tensor_tensor(comb[:, :, :], comb[:, :, :], onehot[:, :, :], ALU.add), m)
        m = dve.do(lambda e: e.tensor_tensor(comb[:, :, :], comb[:, :, :], scores[:, :, :], ALU.mult), m)
        m = dve.do(lambda e: e.tensor_reduce(norm[:, :], comb[:, :, :], AX.X, ALU.add), m)
        m = dve.do(lambda e: e.reciprocal(norm[:, :], norm[:, :]), m)
        m = dve.do(lambda e: e.tensor_tensor(comb[:, :, :], comb[:, :, :],
                                             norm[:, :, None].to_broadcast([P, NT, E]), ALU.mult), m)
        comb_ready = dve.do(lambda e: e.tensor_scalar(comb[:, :, :], comb[:, :, :], ROUTE_SCALE / WS, None, ALU.mult), m)

        SP = [bank[6], bank[7]]
        scan_free = {0: (b0,), 1: (state_bias_ready,)}
        scan = {"tanh": None, "n": 0, "start": None}

        def scan_step(p, j):
            n = scan["n"]
            sp, first = SP[n % 2], p == 0 and j == 0
            a = pe.do(lambda e: e.matmul(sp[:, 0:C], ident_f[:, :], u_sb[:, :, j], start=True, stop=first), idf, u_ready,
                      *scan_free[n % 2])
            if not first:
                h = H[p][:, :, j - 1] if j else start[p - 1][:, :]
                a = pe.do(lambda e: e.matmul(sp[:, 0:C], rec_bd[:, :], h, start=False, stop=True), rec_in,
                          scan["tanh"] if j else scan["start"])
            t = act.do(lambda e: e.activation(H[p][:, :, j], sp[:, 0:C], ACT.Tanh), a)
            scan["tanh"] = t
            scan_free[n % 2] = (t,)
            scan["n"] += 1

        def scan_shift(p):
            n = scan["n"]
            sp = SP[n % 2]
            m = pe.do(lambda e: e.matmul(sp[:, 0:1], shift_f[:, :], H[p][:, C - 1:C, L - 1], start=True, stop=True),
                      shift_ready, scan["tanh"], *scan_free[n % 2])
            a = dve.do(lambda e: e.tensor_copy(start[p][:, 1:C], H[p][:, 0:C - 1, L - 1]), scan["tanh"])
            b = dve.do(lambda e: e.tensor_copy(start[p][:, 0:1], sp[:, 0:1]), m)
            scan_free[n % 2] = (b,)
            scan["n"] += 1
            scan["start"] = b

        def scan_check():
            n = scan["n"]
            sp = SP[n % 2]
            d = dve.do(lambda e: e.tensor_tensor(differ[:, :], start[0][:, :], start[1][:, :], ALU.not_equal), scan["start"])
            d = dve.do(lambda e: e.tensor_reduce(differ_max[:, :], differ[:, :], AX.X, ALU.add), d)
            m = pe.do(lambda e: e.matmul(sp[0:1, 0:1], differ_max[:, :], ones_col[:, :], start=True, stop=True), d,
                      ones_ready[0], *scan_free[n % 2])
            return dve.do(lambda e: e.tensor_copy(flag[:, :], sp[0:1, 0:1]), m)

        scan_work = ([lambda j=j: scan_step(0, j) for j in range(L)] + [lambda: scan_shift(0)]
                     + [lambda j=j: scan_step(1, j) for j in range(L)] + [lambda: scan_shift(1), scan_check])

        GB, UB, YB = [bank[0], bank[1]], [bank[2], bank[3]], [bank[4], bank[5]]
        gu_free = {0: (bank_free[0],) + (bank_free[1],) + (sc,), 1: (bank_free[0], bank_free[1], u_ready)}
        y_free = {0: gate_bank_free[0], 1: gate_bank_free[1]}
        ymark = {}
        h_free, hl_free = {0: (), 1: ()}, {0: (), 1: ()}
        pending = None
        units = [(oe, b) for oe in range(NE) for b in range(NB)]

        def down(unit, n, h_ready):
            oe, b = unit
            e_idx = ORDER[oe]
            s = n % 2
            for half in range(BT // 2):
                yb = YB[half % 2]
                for i2 in range(2):
                    i = half * 2 + i2
                    for j, (ph, pw) in enumerate(((0, 0), (0, 1), (1, 0))):
                        ym = pe.do(lambda e, i=i, i2=i2, j=j, ph=ph, pw=pw, yb=yb:
                                   e.matmul(yb[:, i2 * D:(i2 + 1) * D], h_p[:, s, ph, i * P:(i + 1) * P],
                                            w_part[:, oe % 2, pw, WG:WG + D], start=j == 0, stop=j == 2),
                                   *h_ready, *y_free[half % 2])
                last = None
                for i2 in range(2):
                    t = b * BT + half * 2 + i2
                    yp = yb[:, i2 * D:(i2 + 1) * D]
                    if oe == 0:
                        last = dve.do(lambda e, t=t, yp=yp: e.tensor_scalar(y_sb[:, t, :], yp, 1.0 / WS, None, ALU.mult), ym)
                    else:
                        last = dve.do(lambda e, t=t, yp=yp, c=e_idx: e.scalar_tensor_tensor(
                            out=y_sb[:, t, :], in0=yp, scalar=comb[:, t, c:c + 1], in1=y_sb[:, t, :], op0=ALU.mult,
                            op1=ALU.add), ym, comb_ready, ymark[t])
                    ymark[t] = last
                y_free[half % 2] = (last,)
            h_free[s] = (ym,)
            if b == NB - 1:
                w_used[oe] = (ym,)

        def load_w(oe):
            marks = w_ready[oe - 2] if oe >= 2 else ()
            e = ORDER[oe]
            w_in[oe] = (load(w_stage[:, oe % 2, 0:WG], w13t[:, e, :], f"w13_in{oe}x", *marks),
                        load(w_stage[:, oe % 2, WG:WG + D], w2t[:, e, :], f"w2_in{oe}x", *marks))

        load_w(0)
        split_weights(0)
        for n, (oe, b) in enumerate(units):
            if b == 1 and oe + 1 < NE:
                load_w(oe + 1)
            if b == 3 and oe + 1 < NE:
                split_weights(oe + 1)
            s = n % 2
            for half, bk in ((0, GB[s]), (1, UB[s])):
                first = True
                for k in range(KD):
                    for px, pw in ((0, 0), (0, 1), (1, 0)):
                        m = pe.do(lambda e, half=half, bk=bk, k=k, px=px, pw=pw, oe=oe, b=b, first=first:
                                  e.matmul(bk[:, :], w_part[:, oe % 2, pw, (2 * k + half) * F:(2 * k + half + 1) * F],
                                           xT[:, px, k, b * BW:(b + 1) * BW], start=first,
                                           stop=k == KD - 1 and (px, pw) == (1, 0)),
                                  *w_ready[oe], *xT_ready[b], *gu_free[s])
                        first = False
                if half == 0:
                    sg = act.do(lambda e, bk=bk, s=s: e.activation(silu_f[:, s, :], bk[:, :], ACT.Silu, scale=DESCALE), m,
                                *hl_free[s])
            hf = dve.do(lambda e, bk=bk, s=s: e.scalar_tensor_tensor(out=h_f[:, s, :], in0=bk[:, :], scalar=DESCALE,
                                                                     in1=silu_f[:, s, :], op0=ALU.mult, op1=ALU.mult),
                        m, sg)
            gu_free[s] = (hf,)
            hh = act.do(lambda e, s=s: e.activation(h_p[:, s, 0, :], h_f[:, s, :], ACT.Copy), hf, *h_free[s])
            hl = pool.do(lambda e, s=s: e.tensor_tensor(h_p[:, s, 1, :], h_f[:, s, :], h_p[:, s, 0, :], ALU.subtract), hh)
            hl_free[s] = (hl,)
            if pending:
                down(*pending)
            pending = ((oe, b), n, (hh, hl))
            if scan_work:
                last = scan_work.pop(0)()
                if not scan_work:
                    flag_ready = last
        down(*pending)

        fb = {k: ctx.enter_context(nc.semaphore(f"fb_{k}")) for k in ("sum", "state", "next", "copied", "end_act", "end_dve")}

        def differs(eng):
            eng.wait_ge(flag_ready[0].handle, flag_ready[1])
            return eng.value_load(flag[0:1, 0:1], min_val=0, max_val=P * C)

        def take(eng, s):
            eng.wait_ge(s, 1)
            eng.sem_inc(s, -1)

        PASSES = T // SEQS // L - 1

        def fallback_pe(eng):
            v = differs(eng)
            with eng.If(v != 0):
                with eng.Fori(0, PASSES):
                    for j in range(L):
                        eng.matmul(SP[0][:, 0:C], ident_f[:, :], u_sb[:, :, j], start=True, stop=False)
                        h = H[1][:, :, j - 1] if j else start[1][:, :]
                        eng.matmul(SP[0][:, 0:C], rec_bd[:, :], h, start=False, stop=True).then_inc(fb["sum"], 1)
                        take(eng, fb["state"])
                    eng.matmul(SP[1][:, 0:1], shift_f[:, :], H[1][:, C - 1:C, L - 1], start=True, stop=True)\
                        .then_inc(fb["next"], 1)
                    take(eng, fb["copied"])
                eng.sem_inc(fb["end_act"], 1)
                eng.sem_inc(fb["end_dve"], 1)

        def fallback_act(eng):
            v = differs(eng)
            with eng.If(v != 0):
                with eng.Fori(0, PASSES):
                    for j in range(L):
                        take(eng, fb["sum"])
                        eng.activation(H[1][:, :, j], SP[0][:, 0:C], ACT.Tanh).then_inc(fb["state"], 1)
                take(eng, fb["end_act"])

        def fallback_dve(eng):
            v = differs(eng)
            with eng.If(v != 0):
                with eng.Fori(0, PASSES):
                    take(eng, fb["next"])
                    eng.tensor_copy(start[1][:, 1:C], H[1][:, 0:C - 1, L - 1])
                    eng.tensor_copy(start[1][:, 0:1], SP[1][:, 0:1]).then_inc(fb["copied"], 1)
                take(eng, fb["end_dve"])

        block = ctx.enter_context(nc.Block())
        pe2, act2, dve2, pool2, sync2 = (Queue(s_pe), Queue(s_act), Queue(s_dve), Queue(s_pool), Queue(None))
        hh = act2.do(lambda e: e.activation(H_p[:, 0, :, :], H[1][:, :, :], ACT.Copy, scale=XS), flag_ready)
        hl = dve2.do(lambda e: e.scalar_tensor_tensor(out=H_p[:, 1, :, :], in0=H[1][:, :, :], scalar=XS,
                                                      in1=H_p[:, 0, :, :], op0=ALU.mult, op1=ALU.subtract), hh)
        Hv = [H_p[:, i, :, :].rearrange("p c j -> p (c j)") for i in range(2)]
        fin_free = {0: y_free[0], 1: y_free[1]}
        s_out = sem("out_stored", 16)
        OB = [bank[4], bank[5]]
        for n in range(NT):
            ob, g, i = OB[n % 2], n // BT, n % BT
            for j, (ph, pw) in enumerate(((0, 0), (0, 1), (1, 0))):
                pe2.do(lambda e, j=j, ph=ph, pw=pw, ob=ob, g=g, i=i:
                       e.matmul(ob[:, 0:D], Hv[ph][:, i * P:(i + 1) * P], outw_p[:, pw, g, :], start=j == 0, stop=False),
                       hh, hl, outw_ready, *fin_free[n % 2], quiet=True)
            om = pe2.do(lambda e, ob=ob: e.matmul(ob[:, 0:D], ones_row3[:, :], bias_rows[:, 1, :], start=False, stop=True),
                        bias_ready)
            sg = act2.do(lambda e, n=n: e.activation(y_sb[:, n, :], y_sb[:, n, :], ACT.Silu), ymark[n])
            a = dve2.do(lambda e, n=n, ob=ob: e.scalar_tensor_tensor(out=mix_sb[:, n, :], in0=ob[:, 0:D], scalar=DESCALE,
                                                                     in1=mix_sb[:, n, :], op0=ALU.mult, op1=ALU.mult),
                        om, gate_ready[n])
            fin_free[n % 2] = (a,)
            r = dve2.do(lambda e, n=n: e.tensor_scalar(xn_f[:, n % BT, :], x_sb[:, n, :], mean_var[:, n, 0:1],
                                                       rstd2[:, 0, n:n + 1], ALU.subtract, ALU.mult))
            a = dve2.do(lambda e, n=n: e.scalar_tensor_tensor(out=mix_sb[:, n, :], in0=xn_f[:, n % BT, :], scalar=1.0 / XS,
                                                              in1=mix_sb[:, n, :], op0=ALU.mult, op1=ALU.add), a, r)
            a = pool2.do(lambda e, n=n: e.tensor_tensor(mix_sb[:, n, :], mix_sb[:, n, :], y_sb[:, n, :], ALU.mult), a, sg)
            a = pool2.do(lambda e, n=n: e.tensor_tensor(y_sb[:, n, :], mix_sb[:, n, :], x_sb[:, n, :], ALU.add), a)
            o_view = out.rearrange("(n p) d -> p n d", p=P)
            done = sync2.do(lambda e, n=n: e.dma_start(o_view[:, n, :], y_sb[:, n, :]), a, counter=s_out)
        sync2.do(lambda e: e.wait_ge(done[0].handle, done[1]), quiet=True)

        @block.tensor
        def _(eng):
            pe.emit(eng)
            fallback_pe(eng)
            pe2.emit(eng)

        @block.scalar
        def _(eng):
            act.emit(eng)
            fallback_act(eng)
            act2.emit(eng)

        @block.vector
        def _(eng):
            dve.emit(eng)
            fallback_dve(eng)
            dve2.emit(eng)

        @block.gpsimd
        def _(eng):
            pool.emit(eng)
            pool2.emit(eng)

        @block.sync
        def _(eng):
            sync.emit(eng)
            sync2.emit(eng)


def kernel(**inputs):
    import concourse.bacc as bacc
    from concourse.bass_utils import run_bass_kernel_spmd

    a = {k: np.asarray(v) for k, v in inputs.items()}
    P = 128
    B, S, D = a["L0_attn_x"].shape

    def on_partitions(w):
        return w.reshape(w.shape[0], D // P, P).transpose(2, 1, 0)

    w13 = np.concatenate([a["L0_ffn_w13"], a["L0_ffn_w13_s"][None]])
    w2 = np.concatenate([a["L0_ffn_w2"], a["L0_ffn_w2_s"][None]])
    n_e, gu, _ = w13.shape
    n = a["L0_attn_A"].shape[0]
    arrays = {
        "x": a["L0_attn_x"].reshape(B * S, D),
        "w13t": w13.reshape(n_e, gu, D // P, P).transpose(3, 0, 2, 1).reshape(P, n_e, (D // P) * gu),
        "w2t": w2.transpose(2, 0, 1),
        "router_wt": on_partitions(a["L0_ffn_gate_w"]),
        "router_b": a["L0_ffn_gate_b"][None],
        "gate_wt": on_partitions(a["L0_attn_Wg"]),
        "gate_b_row": a["L0_attn_bg"][None],
        "state_wt": on_partitions(a["L0_attn_Ws"]),
        "input_wt": on_partitions(a["L0_attn_Wi"]),
        "state_b": np.tile(a["L0_attn_bs"], P // n)[:, None],
        "input_b": np.tile(a["L0_attn_bi"], P // n)[:, None],
        "rec_at": a["L0_attn_A"].T,
        "out_wt": np.tile(a["L0_attn_Wo"].T, (P // n, 1)),
        "out_b_row": a["L0_attn_bo"][None],
        "ln_w": a["L0_attn_ln_w"].reshape(D // P, P).T,
        "ln_b": a["L0_attn_ln_b"].reshape(D // P, P).T,
    }
    arrays = {f"in_{k}": np.ascontiguousarray(v) for k, v in arrays.items()}
    nc = bacc.Bacc("TRN2", target_bir_lowering=False, num_devices=1)
    args = [nc.dram_tensor(k, v.shape, mybir.dt.from_np(v.dtype), kind="ExternalInput").ap() for k, v in arrays.items()]
    out = nc.dram_tensor("out", (B * S, D), mybir.dt.float32, kind="ExternalOutput").ap()
    recurrent_gated_moe(nc, *args, out)
    r = run_bass_kernel_spmd(nc, [arrays], core_ids=[0])
    return r.results[0]["out"].reshape(B, S, D)
```

```python
import concourse.bass as bass
from concourse import mybir
from contextlib import ExitStack

import numpy as np


class Counter:

    def __init__(self, handle, unit=1):
        self.handle, self.unit, self.value = handle, unit, 0

    def give(self):
        self.value += self.unit
        return self, self.value


class Queue:

    def __init__(self, counter):
        self.steps, self.counter = [], counter

    def do(self, make, *marks, counter=None, quiet=False):
        mark = None if quiet else (counter or self.counter).give()
        self.steps.append((make, marks, mark))
        return mark

    def emit(self, engine):
        reached = {}
        for make, marks, mark in self.steps:
            for sig, value in marks:
                if reached.get(sig.handle.name, 0) < value:
                    engine.wait_ge(sig.handle, value)
                    reached[sig.handle.name] = value
            instruction = make(engine)
            if mark is not None:
                instruction.then_inc(mark[0].handle, mark[0].unit)


def recurrent_gated_moe(nc: bass.Bass, x, w13t, w2t, router_wt, router_b, gate_wt, gate_b_row, state_wt, input_wt,
                        state_b, input_b, rec_at, out_wt, out_b_row, ln_w, ln_b, out, x_parts_dram, y_dram, ys_dram):
    f32, f16, bf16, i32, u32 = (mybir.dt.float32, mybir.dt.float16, mybir.dt.bfloat16, mybir.dt.int32,
                                mybir.dt.uint32)
    ALU, ACT, AX = mybir.AluOpType, mybir.ActivationFunctionType, mybir.AxisListType

    P = 128
    T, D = x.shape
    KD = D // P
    NT = T // P
    E = router_wt.shape[2]
    N = rec_at.shape[0]
    F = w2t.shape[0]
    TOPK = 4
    ROUTE_SCALE = 2.5
    EPS = 1e-5
    BT = 4
    NB = NT // BT
    BW = BT * P
    G = P // N
    L = 16
    C = BW // L
    SEQS = 2
    XS, WS = 16.0, 64.0
    DESCALE = 1.0 / (XS * WS)
    NBLK = T * TOPK // P + E
    NPAIR = NBLK // 2
    WG, W2 = KD * 2 * F, D
    WE = 2 * WG + 2 * W2
    STAGES = 4
    SPLIT3 = ((0, 0), (0, 1), (1, 0))

    ctx = ExitStack()
    with ctx:
        def sb(name, shape, dt=f32):
            return ctx.enter_context(nc.sbuf_tensor(name, shape, dt))

        def sem(name, unit=1):
            return Counter(ctx.enter_context(nc.semaphore(name)), unit)

        x_sb = sb("x_sb", [P, NT, D])
        mix_sb = sb("mix_sb", [P, NT, D])
        w_all = sb("w_all", [P, E, WE], f16)
        w_shared = sb("w_shared", [P, WE], f16)
        w_stage = sb("w_stage", [P, STAGES, WG + W2])
        xT = sb("xT", [P, 2, KD, T], f16)
        xn_f = sb("xn_f", [P, BT, D])
        xn_parts = sb("xn_parts", [P, 2, BT, 2, D], f16)
        zn_f = sb("zn_f", [P, BT, D])
        zn_parts = sb("zn_parts", [P, BT, 2, D], f16)
        zT = sb("zT", [P, 2, KD, BW], f16)
        mean_var = sb("mean_var", [P, NT, 2])
        var2 = sb("var2", [P, 2, NT])
        root2 = sb("root2", [P, 2, NT])
        newton = sb("newton", [P, 2, NT])
        rstd2 = sb("rstd2", [P, 2, NT])
        ident_f = sb("ident_f", [P, P])
        ident_h = sb("ident_h", [P, P], f16)
        shift_f = sb("shift_f", [P, P])
        before_h = sb("before_h", [P, P], f16)
        ones_h = sb("ones_h", [P, P], f16)
        tri_h = sb("tri_h", [E, 2, E], f16)
        ones_col = sb("ones_col", [P, 1])
        ones_row3 = sb("ones_row3", [3, P], bf16)
        lnw_sb = sb("lnw_sb", [P, KD])
        lnb_sb = sb("lnb_sb", [P, KD])
        router_f = sb("router_f", [P, KD, E])
        router_p = sb("router_p", [P, 2, KD, E], f16)
        router_bias = sb("router_bias", [P, E])
        gate_p = sb("gate_p", [P, 2, KD, D], f16)
        state_pad = sb("state_pad", [P, 2, KD, 2 * P - N], f16)
        sbias = sb("sbias", [P, 2])
        state_bias = sb("state_bias", [P, 1])
        rec_bd = sb("rec_bd", [P, P])
        bias_rows = sb("bias_rows", [3, 2, D], bf16)
        u_sb = sb("u_sb", [P, C, L])
        H = [sb(f"H{i}", [P, C, L]) for i in range(2)]
        H_p = sb("H_p", [P, 2, C, L], f16)
        start = [sb(f"start{i}", [P, C]) for i in range(2)]
        differ = sb("differ", [P, C])
        differ_max = sb("differ_max", [P, 1])
        flag = sb("flag", [1, 1], i32)
        topk_w = sb("topk_w", [P, NT, TOPK])
        token_of = sb("token_of", [P, NBLK], u32)
        row_of = sb("row_of", [P, NBLK], u32)
        expert_of = sb("expert_of", [1, NBLK], i32)
        hT_sb = sb("hT_sb", [P, 2, 2, 2, P], f16)
        h_parts = sb("h_parts", [P, 2, 2, 2, F], f16)
        iota_blk = sb("iota_blk", [P, NBLK], f16)

        scratch, at = mix_sb[:, :, :].rearrange("p n d -> p (n d)"), [0]

        def scratch_of(width, pattern=None, dt=f32, rows=P, **dims):
            v = scratch[0:rows, at[0]:at[0] + width]
            at[0] += width
            assert at[0] <= NT * D
            v = v if dt is f32 else v.bitcast(dt)
            return v.rearrange(pattern, **dims) if pattern else v

        iota_4 = scratch_of(NBLK * TOPK // 2, "p (s k) -> p s k", dt=f16, k=TOPK)
        scores = scratch_of(NT * E, "p (n e) -> p n e", e=E)
        idx_h = scratch_of(NT * TOPK // 2, "p (n k) -> p n k", dt=f16, k=TOPK)
        chosen = scratch_of(TOPK * NT * E // 2, "p (n k e) -> p n k e", dt=f16, k=TOPK, e=E)
        chosen_any = scratch_of(NT * E // 2, "p (n e) -> p n e", dt=f16, e=E)
        chosen_2 = scratch_of(BT * E, "p (n k e) -> p n k e", dt=f16, n=BT, k=2)
        chosen_batch = scratch_of(E // 2, dt=f16)
        chosen_before = scratch_of((NB + 1) * E // 2, "p (b e) -> p b e", dt=f16, e=E)
        slot_e = scratch_of(NT * E, "p (n e) -> p n e", e=E)
        slot_f = scratch_of(NT * TOPK, "p (n k) -> p n k", k=TOPK)
        slot_i = scratch_of(NT * TOPK, dt=i32)
        part_i = scratch_of(2 * NT * TOPK, "p (i n) -> p i n", dt=i32, i=2)
        slot_lo = scratch_of(NT * TOPK // 2, "p (n k) -> p n k", dt=f16, k=TOPK)
        entry_h = scratch_of(NT * TOPK // 2, "p (n k) -> p n k", dt=f16, k=TOPK)
        slot_hi = scratch_of(NT * TOPK // 2, "p (n k) -> p n k", dt=f16, k=TOPK)
        entry = scratch_of(NT * TOPK, "p (n k) -> p n k", k=TOPK)
        norm = scratch_of(NT)
        count_i = scratch_of(2, dt=i32)
        nblk_f = scratch_of(1)
        nblk_h = scratch_of(P // 2, dt=f16)
        blk_end = scratch_of(1)
        blk_start = scratch_of(E)
        ended = scratch_of(NBLK)
        pad_row = scratch_of(NBLK)
        stats = scratch_of(NT * 6, "p (n i) -> p n i", i=6)
        empty = scratch_of(NBLK)
        rows_f = scratch_of(NBLK)
        rows_i = scratch_of(NBLK, dt=i32)
        picked_at = at[0]
        biased = scratch_of(NT * E, "p (n e) -> p n e", e=E)
        top8 = scratch_of(NT * 8, "p (n e) -> p n e", e=8)
        idx8 = scratch_of(NT * 8, "p (n e) -> p n e", dt=u32, e=8)
        at[0] = picked_at
        picked = scratch_of(NT * TOPK * E, "p (n k e) -> p n k e", k=TOPK, e=E)
        at[0] = picked_at
        HOT_RING = 5
        lo_hot = scratch_of(HOT_RING * TOPK * P // 2, "p (r s k) -> p r s k", dt=f16, r=HOT_RING, k=TOPK)
        hi_hot = scratch_of(HOT_RING * TOPK * NBLK // 2, "p (r s k) -> p r s k", dt=f16, r=HOT_RING, k=TOPK)

        stage = [w_stage[:, i, :] for i in range(STAGES)]
        stages, used = w_stage[:, :, :].rearrange("p s w -> p (s w)"), [0]

        def stage_of(width, pattern=None, **dims):
            v = stages[:, used[0]:used[0] + width]
            used[0] += width
            assert used[0] <= STAGES * (WG + W2)
            return v.rearrange(pattern, **dims) if pattern else v

        gate_f = stage_of(KD * D, "p (k d) -> p k d", k=KD)
        state_f = stage_of(2 * KD * N, "p (i k n) -> p i k n", i=2, k=KD)
        state_rep = stage_of(KD * G * N, "p (k g n) -> p k g n", k=KD, g=G)
        state_sum = stage_of(KD * N, "p (k n) -> p k n", k=KD)
        state_w = stage_of(KD * N, "p (k n) -> p k n", k=KD)
        bias_in = stage_of(2 * D, "p (b d) -> p b d", b=2)[0:1]
        bias_f = stage_of(2 * D, "p (b d) -> p b d", b=2)[0:1]
        bias_part = stage_of(3 * D)[0:1].bitcast(bf16).rearrange("p (j b d) -> p j b d", j=3, b=2)

        sh_silu = xn_parts[:, 0, 0:2, :, :].rearrange("p b i d -> p (b i d)").bitcast(f32)
        sh_h = xn_parts[:, 0, 2:4, :, :].rearrange("p b i d -> p (b i d)").bitcast(f32)
        sh_parts = xn_parts[:, 1, 0:2, :, :].rearrange("p b i d -> p b (i d)")
        sh_y = xn_f[:, :, :].rearrange("p (s b) d -> p s b d", s=2)
        PW = 2 * 2 * D
        xg_T = xn_parts[:, 0, :, :, :].rearrange("p b i d -> p (b i d)").rearrange("p (s w) -> p s w", w=PW)
        silu_sb = xn_parts[:, 1, 0:2, :, :].rearrange("p b i d -> p (b i d)").bitcast(f32)\
            .rearrange("p (s b f) -> p s b f", s=2, b=2)
        h_sb = xn_parts[:, 1, 2:4, :, :].rearrange("p b i d -> p (b i d)").bitcast(f32)\
            .rearrange("p (s b f) -> p s b f", s=2, b=2)
        XG_RING, YS_RING = 6, 4
        xT_flat = xT[:, :, :, :].rearrange("p i k t -> p (i k t)")
        x_ring = xT_flat[:, 0:XG_RING * PW].rearrange("p (r b w) -> p r b w", r=XG_RING, b=2)
        y_at = XG_RING * PW
        y_ring = xT_flat[:, y_at:y_at + YS_RING * 4 * D].bitcast(f32).rearrange("p (r b d) -> p r b d", r=YS_RING, b=2)
        o_at = y_at + YS_RING * 4 * D
        outw_p = xT_flat[:, o_at:o_at + 2 * G * D].rearrange("p (i g d) -> p i g d", i=2, g=G)
        outw_c = zn_f[:, 0, :].bitcast(f16).rearrange("p (i d) -> p i d", i=2)
        FIN_RING = 8
        fin_ring = w_all[:, :, :].rearrange("p e w -> p (e w)")[:, 0:FIN_RING * 2 * (TOPK + 1) * D].bitcast(f32)\
            .rearrange("p (r k d) -> p r k d", r=FIN_RING, k=TOPK + 1)

        bank = [ctx.enter_context(nc.psum_tensor(f"bank{i}", [P, 512], f32)) for i in range(8)]

        s_pe, s_act, s_dve, s_pool = sem("pe_done"), sem("act_done"), sem("dve_done"), sem("pool_done")
        pe, act, dve, pool, sync = Queue(s_pe), Queue(s_act), Queue(s_dve), Queue(s_pool), Queue(None)

        def load(dst, src, name, *marks, queue=None):
            return (queue or sync).do(lambda e: e.dma_start(dst, src), *marks, counter=sem(name, 16))

        XL = 4
        x_view = x.rearrange("(n p) d -> p n d", p=P)
        x_in = [load(x_sb[:, n:n + XL, :], x_view[:, n:n + XL, :], f"x_in{n}") for n in range(0, NT, XL)]
        router_in = load(router_f[:, :, :], router_wt, "router_in", queue=act)
        rb_in = load(router_bias[:, :], router_b.broadcast_to([P, E]), "rb_in", queue=act)
        lnw_in = load(lnw_sb[:, :], ln_w, "lnw_in", queue=act)
        lnb_in = load(lnb_sb[:, :], ln_b, "lnb_in", queue=act)
        sb_in = load(sbias[:, 0:1], state_b, "sb_in", queue=act)
        ib_in = load(sbias[:, 1:2], input_b, "ib_in", queue=act)

        def diagonal(t, fill_base, zeroed, width=P):
            return pool.do(lambda e: e.affine_select(out=t, in_=t, compare_op=ALU.not_equal, fill=1.0, base=fill_base,
                                                     pattern=[[-1, width]], channel_multiplier=1), zeroed)

        z = [pool.do(lambda e, t=t: e.memset(t, 0.0)) for t in
             (ident_h[:, :], ident_f[:, :], shift_f[:, :], rec_bd[:, :], state_pad[:, :, :, :])]
        idh = diagonal(ident_h[:, :], 0, z[0])
        idf = diagonal(ident_f[:, :], 0, z[1])
        sh0 = diagonal(shift_f[:, :], N, z[2])
        shift_ready = pool.do(lambda e: e.memset(shift_f[:, P // SEQS:P // SEQS + N], 0.0), sh0)
        ones_ready = [pool.do(lambda e, t=t: e.memset(t, 1.0)) for t in
                      (ones_col[:, :], ones_row3[:, :], ones_h[:, :], before_h[:, :], tri_h[:, :, :])]
        before_ready = pool.do(lambda e: e.affine_select(out=before_h[:, :], in_=before_h[:, :], compare_op=ALU.is_gt,
                                                         fill=0.0, base=0, pattern=[[1, P]], channel_multiplier=-1),
                               ones_ready[3])
        for j, cmp in enumerate((ALU.is_ge, ALU.is_gt)):
            tri_ready = pool.do(lambda e, j=j, cmp=cmp: e.affine_select(
                out=tri_h[:, j, :], in_=tri_h[:, j, :], compare_op=cmp, fill=0.0, base=0, pattern=[[1, E]],
                channel_multiplier=-1), ones_ready[4])
        iota_e = iota_blk[:, 0:E]
        ROW_SHIFT, ROW_BASE = 13, 127 << 10

        def iota(t, pattern, base, step):
            return pool.do(lambda e: e.iota(t, pattern=pattern, base=base, channel_multiplier=step,
                                            allow_small_or_imprecise_dtypes=True))

        iotas = [iota(iota_4[:, :, :], [[1, NBLK], [0, TOPK]], 0, 0), iota(iota_blk[:, :], [[1, NBLK]], 0, 0),
                 iota(entry[:, :, :].bitcast(i32), [[P * TOPK, NT], [1, TOPK]], ROW_BASE, TOPK),
                 iota(pad_row[:, :], [[P, NBLK]], T * TOPK + ROW_BASE, 1)]
        entry_ready = dve.do(lambda e: e.tensor_scalar(entry[:, :, :].bitcast(i32), entry[:, :, :].bitcast(i32), ROW_SHIFT,
                                                       None, ALU.logical_shift_left), iotas[2])
        entry_ready = dve.do(lambda e: e.tensor_copy(entry_h[:, :, :], entry[:, :, :]), entry_ready)
        s_bd = sem("rec_in", 16)
        for g in range(G):
            rec_in = sync.do(lambda e, g=g: e.dma_start(rec_bd[g * N:(g + 1) * N, g * N:(g + 1) * N], rec_at), z[3],
                             counter=s_bd)

        r_hi = dve.do(lambda e: e.tensor_scalar(router_p[:, 0, :, :], router_f[:, :, :], WS, None, ALU.mult), router_in)
        r_lo = dve.do(lambda e: e.scalar_tensor_tensor(out=router_p[:, 1, :, :], in0=router_f[:, :, :], scalar=WS,
                                                       in1=router_p[:, 0, :, :], op0=ALU.mult, op1=ALU.subtract), r_hi)

        stage_free, w_ready, staged = [()] * STAGES, {}, {}
        s_w13 = [sem(f"w13_in{i}", 16) for i in range(STAGES)]
        s_w2 = [sem(f"w2_in{i}", 16) for i in range(STAGES)]
        ORDER_E = (E, *range(E))

        def load_weights(n):
            e_idx, i = ORDER_E[n], n % STAGES
            staged[n] = (
                sync.do(lambda q: q.dma_start(stage[i][:, 0:WG], w13t[:, e_idx, :]), *stage_free[i], counter=s_w13[i]),
                sync.do(lambda q: q.dma_start(stage[i][:, WG:WG + W2], w2t[:, e_idx, :]), *stage_free[i], counter=s_w2[i]))

        def split_weights(n):
            e_idx, st = ORDER_E[n], stage[n % STAGES]
            dst = w_shared[:, :] if e_idx == E else w_all[:, e_idx, :]
            marks = []
            for hi, lo, src in ((dst[:, 0:WG], dst[:, WG:2 * WG], st[:, 0:WG]),
                                (dst[:, 2 * WG:2 * WG + W2], dst[:, 2 * WG + W2:WE], st[:, WG:WG + W2])):
                w = act.do(lambda q, src=src: q.activation(src, src, ACT.Copy, scale=WS), *staged[n])
                h = act.do(lambda q, hi=hi, src=src: q.activation(hi, src, ACT.Copy), w)
                marks.append(pool.do(lambda q, hi=hi, lo=lo, src=src: q.tensor_tensor(lo, src, hi, ALU.subtract), h))
            stage_free[n % STAGES], w_ready[e_idx] = (marks[1],), (h, marks[1])
            if n + STAGES <= E:
                load_weights(n + STAGES)

        for n in range(STAGES):
            load_weights(n)

        SB = NT // 4
        rstd_ready, stats_of = [], {}

        def norm_stats(q):
            r = slice(q * SB, (q + 1) * SB)
            for n in range(q * SB, (q + 1) * SB):
                st = dve.do(lambda e, n=n: e.bn_stats(stats[:, n, :], x_sb[:, n, :]), x_in[n // XL])
            for n in range(q * SB, (q + 1) * SB):
                mv = dve.do(lambda e, n=n: e.bn_aggr(mean_var[:, n, :], stats[:, n, :]), st)
            v = mean_var[:, r, 1]
            a = dve.do(lambda e: e.tensor_scalar(var2[:, 0, r], v, 1.0, EPS, ALU.mult, ALU.add), mv)
            b = dve.do(lambda e: e.tensor_scalar(var2[:, 1, r], v, 1.0 + EPS, EPS * EPS, ALU.mult, ALU.add), mv)
            stats_of[q] = act.do(lambda e: e.activation(root2[:, :, r], var2[:, :, r], ACT.Sqrt), a, b)

        def norm_scale(q):
            r = slice(q * SB, (q + 1) * SB)
            y = dve.do(lambda e: e.reciprocal(rstd2[:, :, r], root2[:, :, r]), stats_of[q])
            y = dve.do(lambda e: e.tensor_tensor(newton[:, :, r], rstd2[:, :, r], rstd2[:, :, r], ALU.mult), y)
            y = dve.do(lambda e: e.tensor_tensor(newton[:, :, r], newton[:, :, r], var2[:, :, r], ALU.mult), y)
            y = dve.do(lambda e: e.tensor_scalar(newton[:, :, r], newton[:, :, r], -0.5 * XS, 1.5 * XS, ALU.mult, ALU.add), y)
            rstd_ready.append(dve.do(lambda e: e.tensor_tensor(rstd2[:, :, r], rstd2[:, :, r], newton[:, :, r], ALU.mult), y))

        TP = [bank[0], bank[1]]
        tp = {"n": 0, "free": [(), ()]}

        def transposed(src_of, dst, ready, engine, *extra):
            s = tp["n"] % 2
            tb = TP[s][:, :].bitcast(f16)
            for j in range(2 * BT):
                t = pe.do(lambda e, j=j: e.transpose(tb[:, j * P:(j + 1) * P], src_of(j), ident_h[:, :]),
                          idh, *ready, *tp["free"][s], quiet=j < 2 * BT - 1)
            view = tb.rearrange("p (k t) -> p k t", k=KD) if len(dst.shape) == 3 else tb
            copy = (lambda e: e.activation(dst, view, ACT.Copy)) if engine is act else (lambda e: e.tensor_copy(dst, view))
            ev = engine.do(copy, t, *extra)
            tp["free"][s], tp["n"] = (ev,), tp["n"] + 1
            return t, ev

        ROUTE = [bank[2], bank[7]]
        parts_free, xf_free, xT_ready, xp_out, xn_made = [(), ()], [(), ()], {}, [], {}
        s_xp = [sem(f"x_parts_out{i}", 16) for i in range(2)]
        xp_view = x_parts_dram.rearrange("(n p) (i d) -> p n i d", p=P, i=2)

        def x_norm(b):
            ready, s = rstd_ready[b * BT // SB], b % 2
            xf = (xn_f, zn_f)[s]
            for i in range(BT):
                nx = dve.do(lambda e, n=b * BT + i, i=i: e.tensor_scalar(xf[:, i, :], x_sb[:, n, :], mean_var[:, n, 0:1],
                                                                         rstd2[:, 0, n:n + 1], ALU.subtract, ALU.mult),
                            ready, *xf_free[s])
            xh = act.do(lambda e: e.activation(xn_parts[:, s, :, 0, :], xf[:, :, :], ACT.Copy), nx, *parts_free[s])
            xl = pool.do(lambda e: e.tensor_tensor(xn_parts[:, s, :, 1, :], xf[:, :, :], xn_parts[:, s, :, 0, :],
                                                   ALU.subtract), xh, *parts_free[s])
            xf_free[s], xn_made[b] = (xl,), (xh, xl)
            xp_out.append(sync.do(lambda e: e.dma_start(xp_view[:, b * BT:(b + 1) * BT, :, :], xn_parts[:, s, :, :, :]), xl,
                                  counter=s_xp[s]))

        def x_transpose(b):
            s, made = b % 2, []
            for part in range(2):
                t, ev = transposed(lambda j, part=part: xn_parts[:, s, j % BT, part, (j // BT) * P:(j // BT + 1) * P],
                                   xT[:, part, :, b * BW:(b + 1) * BW], (xn_made[b][part],), dve if part else act)
                made.append(ev)
            parts_free[s] = (t, xp_out[b])
            xT_ready[b] = tuple(made)

        R, RANK = {"scored": {}}, bank[3]

        def route_batch(b):
            cols = slice(b * BT * E, (b + 1) * BT * E)
            order = [(pa, pw, k) for k in range(KD) for pa in range(2) for pw in range(2)]
            for n in range(b * BT, (b + 1) * BT):
                for j, (pa, pw, k) in enumerate(order):
                    rt = pe.do(lambda e, n=n, j=j, pa=pa, pw=pw, k=k:
                               e.matmul(ROUTE[b % 2][:, n * E:(n + 1) * E], xT[:, pa, k, n * P:(n + 1) * P],
                                        router_p[:, pw, k, :], start=j == 0, stop=j == len(order) - 1),
                               *xT_ready[b], r_lo, *R["scored"].get(b - 2, ()), quiet=j < len(order) - 1)
            R["sc"] = act.do(lambda e: e.activation(scores[:, :, :].rearrange("p n e -> p (n e)")[:, cols], ROUTE[b % 2][:, cols],
                                                    ACT.Sigmoid, scale=DESCALE), rt)
            R["scored"][b] = (R["sc"],)

        def choose_batch(b):
            r, first = slice(b * BT, (b + 1) * BT), b * BT
            bi = dve.do(lambda e: e.tensor_tensor(biased[:, r, :], scores[:, r, :],
                                                  router_bias[:, None, :].to_broadcast([P, BT, E]), ALU.add),
                        *R["scored"][b], rb_in)
            for n in range(first, first + BT):
                mx = dve.do(lambda e, n=n: e.max(top8[:, n, :], biased[:, n, :]), bi)
            for n in range(first, first + BT):
                ix = dve.do(lambda e, n=n: e.max_index(idx8[:, n, :], top8[:, n, :], biased[:, n, :]), mx)
            m = dve.do(lambda e: e.tensor_copy(idx_h[:, r, :], idx8[:, r, 0:TOPK]), ix)
            m = dve.do(lambda e: e.tensor_tensor(
                chosen[:, r, :, :].rearrange("p n k e -> p (n k) e"),
                idx_h[:, r, :].rearrange("p n k -> p (n k)")[:, :, None].to_broadcast([P, BT * TOPK, E]),
                iota_e[:, None, :].to_broadcast([P, BT * TOPK, E]), ALU.is_equal), m, iotas[1])
            def add(out_, a, c, *marks):
                return dve.do(lambda e: e.tensor_tensor(out_, a, c, ALU.add), *marks)

            m = add(chosen_2[:, :, :, :], chosen[:, r, 0:2, :], chosen[:, r, 2:4, :], m)
            any_ = add(chosen_any[:, r, :], chosen_2[:, :, 0, :], chosen_2[:, :, 1, :], m)
            m = add(chosen_2[:, 0:2, 0, :], chosen_any[:, first:first + 2, :], chosen_any[:, first + 2:first + 4, :], any_)
            m = add(chosen_batch if b else chosen_before[:, 1, :], chosen_2[:, 0, 0, :], chosen_2[:, 1, 0, :], m)
            if b:
                m = add(chosen_before[:, b + 1, :], chosen_before[:, b, :], chosen_batch, m)
            R["before", b + 1], R["any", b] = m, any_

        def rank_batch(b):
            first = b * BT
            out_of = RANK[:, first * E:(first + BT) * E]
            pe.do(lambda e: e.matmul(out_of, before_h[:, :], chosen_any[:, first:first + BT, :].rearrange("p n e -> p (n e)"),
                                     start=True, stop=False), R["any", b], before_ready, quiet=True)
            if b:
                pe.do(lambda e: e.matmul(out_of.rearrange("p (t e) -> p t e", e=E), ones_h[:, :],
                                         chosen_before[:, b:b + 1, :].to_broadcast([P, BT, E]), start=False, stop=False),
                      R["before", b], ones_ready[2], quiet=True)
            for i in range(BT - 1):
                R["rank"] = pe.do(lambda e, i=i: e.matmul(
                    RANK[:, (first + i + 1) * E:(first + BT) * E].rearrange("p (t e) -> p t e", e=E), ones_h[:, :],
                    chosen_any[:, first + i:first + i + 1, :].to_broadcast([P, BT - 1 - i, E]), start=False,
                    stop=i == BT - 2), ones_ready[2], quiet=i < BT - 2)

        SG, SU, SY = bank[4], bank[5], [bank[0], bank[1]]
        shared = {"free": [(), ()], "up_free": (), "parts_read": (), "h": (), "y_free": [(), ()], "out": []}
        s_sy = [sem(f"shared_y_out{i}", 16) for i in range(2)]
        ysh_view = ys_dram.rearrange("(n p) d -> p n d", p=P)

        def shared_up(b):
            for half, bk in ((0, SG), (1, SU)):
                steps = [(k, px, pw) for k in range(KD) for px, pw in SPLIT3]
                for j, (k, px, pw) in enumerate(steps):
                    m = pe.do(lambda e, half=half, bk=bk, j=j, k=k, px=px, pw=pw:
                              e.matmul(bk[:, :], w_shared[:, pw * WG + (2 * k + half) * F:pw * WG + (2 * k + half + 1) * F],
                                       xT[:, px, k, b * BW:(b + 1) * BW], start=j == 0, stop=j == len(steps) - 1),
                              *w_ready[E], *xT_ready[b], *shared["up_free"], quiet=j < len(steps) - 1)
                if half == 0:
                    sg = act.do(lambda e: e.activation(sh_silu, SG[:, :], ACT.Silu, scale=DESCALE), m, *shared["up_free"], *xp_out[-2:])
            shared["up"] = (m, sg)

        def shared_hidden(b):
            m, sg = shared["up"]
            hf = dve.do(lambda e: e.scalar_tensor_tensor(out=sh_h, in0=SU[:, :], scalar=DESCALE, in1=sh_silu,
                                                         op0=ALU.mult, op1=ALU.mult), m, sg, *shared["h"])
            shared["up_free"] = (hf,)
            hh = act.do(lambda e: e.activation(sh_parts[:, 0, :], sh_h, ACT.Copy), hf, *shared["parts_read"])
            shared["h"] = (hh, pool.do(lambda e: e.tensor_tensor(sh_parts[:, 1, :], sh_h, sh_parts[:, 0, :], ALU.subtract),
                                       hh))

        def shared_down(b):
            for half, bk in enumerate(SY):
                for i2 in range(2):
                    i = half * 2 + i2
                    for j, (ph, pw) in enumerate(SPLIT3):
                        m = pe.do(lambda e, i=i, i2=i2, j=j, ph=ph, pw=pw, bk=bk:
                                  e.matmul(bk[:, i2 * D:(i2 + 1) * D], sh_parts[:, ph, i * P:(i + 1) * P],
                                           w_shared[:, 2 * WG + pw * W2:2 * WG + (pw + 1) * W2], start=j == 0,
                                           stop=j == 2), *shared["h"], *tp["free"][0], *tp["free"][1],
                                  *shared["free"][half], quiet=not (i2 == 1 and j == 2))
                ev = act.do(lambda e, half=half, bk=bk: e.activation(sh_y[:, half, :, :],
                                                                     bk[:, :].rearrange("p (b d) -> p b d", b=2),
                                                                     ACT.Copy, scale=1.0 / WS), m,
                            *shared["y_free"][half], *xf_free[0])
                o = sync.do(lambda e, half=half: e.dma_start(ysh_view[:, b * BT + half * 2:b * BT + half * 2 + 2, :],
                                                             sh_y[:, half, :, :]), ev, counter=s_sy[half])
                shared["y_free"][half] = (o,)
                shared["free"][half] = (ev,)
            shared["last"], shared["parts_read"] = m, (m,)

        norm_stats(0)
        norm_stats(1)
        norm_scale(0)
        for b in range(NB + 3):
            if b < NB:
                x_norm(b)
            if b < 2:
                norm_stats(b + 2)
            if b < 3:
                norm_scale(b + 1)
            if 0 <= b - 1 < NB:
                x_transpose(b - 1)
            if 0 <= b - 2 < NB:
                route_batch(b - 2)
            if b < NB:
                split_weights(b)
            if 0 <= b - 4:
                rank_batch(b - 4)
            if b == NB + 2:
                shared_up(0)
            if 0 <= b - 3 < NB:
                choose_batch(b - 3)
        shared_hidden(0)
        rank_batch(NB - 1)

        SMALL, TABLE = bank[6], bank[7]

        def route_blocks():
            c = pe.do(lambda e: e.matmul(SMALL[0:E, 0:1], chosen_before[:, NB, :], ones_h[:, 0:1], start=True, stop=True),
                      R["before", NB])
            m = dve.do(lambda e: e.tensor_scalar(count_i[0:E, 0:1], SMALL[0:E, 0:1], float(P - 1), None, ALU.add), c)
            m = dve.do(lambda e: e.tensor_scalar(count_i[0:E, 1:2], count_i[0:E, 0:1], 7, None,
                                                 ALU.arith_shift_right), m)
            m = dve.do(lambda e: e.tensor_copy(nblk_f[0:E, :], count_i[0:E, 1:2]), m)
            nb = dve.do(lambda e: e.tensor_copy(nblk_h[0:E, :], nblk_f[0:E, 0:1].to_broadcast([E, P])), m)
            pe.do(lambda e: e.matmul(SMALL[:, 32:32 + E], nblk_h[0:E, :], tri_h[:, 1, :], start=True, stop=True), nb,
                  tri_ready, quiet=True)
            be = pe.do(lambda e: e.matmul(SMALL[0:E, 64:65], tri_h[:, 0, :], nblk_h[0:E, 0:1], start=True, stop=True))
            bs = dve.do(lambda e: e.tensor_copy(blk_start[:, :], SMALL[:, 32:32 + E]), be)
            be = dve.do(lambda e: e.tensor_copy(blk_end[0:E, :], SMALL[0:E, 64:65]), be)
            R["slot_e"] = dve.do(lambda e: e.scalar_tensor_tensor(
                out=slot_e[:, :, :], in0=blk_start[:, None, :].to_broadcast([P, NT, E]), scalar=float(P),
                in1=RANK[:, :].rearrange("p (n e) -> p n e", e=E), op0=ALU.mult, op1=ALU.add), bs, R["rank"])
            d = dve.do(lambda e: e.tensor_scalar(ended[0:E, :], iota_blk[0:E, :], blk_end[0:E, 0:1], None, ALU.is_ge), be)
            R["eb"] = pe.do(lambda e: e.matmul(SMALL[0:1, 128:128 + NBLK], ones_col[0:E, :], ended[0:E, :], start=True,
                                               stop=True), d, ones_ready[0])

        def pick(dst, src, ready):
            m = dve.do(lambda e: e.tensor_tensor(picked[:, :, :, :], chosen[:, :, :, :],
                                                 src[:, :, None, :].to_broadcast([P, NT, TOPK, E]), ALU.mult), ready)
            return dve.do(lambda e: e.tensor_reduce(dst[:, :, :].rearrange("p n k -> p (n k)"),
                                                    picked[:, :, :, :].rearrange("p n k e -> p (n k) e"), AX.X, ALU.add), m)

        def route_slots():
            m = pick(slot_f, slot_e[:, :, :], R["slot_e"])
            m = dve.do(lambda e: e.tensor_copy(slot_i, slot_f[:, :, :].rearrange("p n k -> p (n k)")), m)
            a = dve.do(lambda e: e.tensor_scalar(part_i[:, 0, :], slot_i, P - 1, None, ALU.bitwise_and), m)
            b = dve.do(lambda e: e.tensor_scalar(part_i[:, 1, :], slot_i, 7, None, ALU.arith_shift_right), m)
            dve.do(lambda e: e.tensor_copy(slot_lo[:, :, :].rearrange("p n k -> p (n k)"), part_i[:, 0, :]), a)
            R["slots"] = dve.do(lambda e: e.tensor_copy(slot_hi[:, :, :].rearrange("p n k -> p (n k)"), part_i[:, 1, :]), b)

        hot_free = [()] * HOT_RING

        def table_tile(n):
            r = n % HOT_RING

            def each(src, width):
                return src[:, n, None, :].to_broadcast([P, width, TOPK])

            hi = dve.do(lambda e: e.tensor_tensor(hi_hot[:, r, :, :], iota_4[:, :, :], each(slot_hi, NBLK), ALU.is_equal),
                        R["slots"], iotas[0], *hot_free[r])
            lo = dve.do(lambda e: e.tensor_tensor(lo_hot[:, r, :, :], iota_4[:, 0:P, :], each(slot_lo, P), ALU.is_equal),
                        R["slots"], *hot_free[r])
            lo = dve.do(lambda e: e.tensor_tensor(lo_hot[:, r, :, :], lo_hot[:, r, :, :], each(entry_h, P), ALU.mult), lo,
                        entry_ready)
            for k in range(TOPK):
                m = pe.do(lambda e, k=k: e.matmul(TABLE[:, 0:NBLK], lo_hot[:, r, :, k], hi_hot[:, r, :, k],
                                                  start=n == 0 and k == 0, stop=n == NT - 1 and k == TOPK - 1),
                          hi, lo, quiet=k < TOPK - 1)
            hot_free[r] = (m,)
            R["table"] = m

        def finish_table():
            m = dve.do(lambda e: e.tensor_copy(rows_f[:, :], TABLE[:, 0:NBLK]), R["table"])
            a = dve.do(lambda e: e.scalar_tensor_tensor(out=empty[:, :], in0=rows_f[:, :], scalar=0.0, in1=pad_row[:, :],
                                                        op0=ALU.is_equal, op1=ALU.mult), m, iotas[3])
            m = dve.do(lambda e: e.tensor_scalar(rows_i[:, :], rows_f[:, :].bitcast(i32), ROW_SHIFT, None,
                                                 ALU.logical_shift_right), m)
            m = dve.do(lambda e: e.tensor_tensor(rows_f[:, :], empty[:, :], rows_i[:, :], ALU.add), m, a)
            R["rows"] = dve.do(lambda e: e.tensor_scalar(row_of[:, :], rows_f[:, :], -float(ROW_BASE), None, ALU.add), m)
            m = dve.do(lambda e: e.tensor_scalar(rows_i[:, :], rows_f[:, :], -float(ROW_BASE), float(T * TOPK - 1), ALU.add,
                                                 ALU.min), m)
            R["tokens"] = dve.do(lambda e: e.tensor_scalar(token_of[:, :].bitcast(i32), rows_i[:, :], 2, None,
                                                           ALU.arith_shift_right), m)
            R["experts"] = dve.do(lambda e: e.tensor_scalar(expert_of[:, :], SMALL[0:1, 128:128 + NBLK], float(E - 1),
                                                            None, ALU.min), R["eb"])

        def pick_weights(i):
            q = NT // 4
            r = slice(i * q, (i + 1) * q)
            m = dve.do(lambda e: e.tensor_tensor(picked[:, r, :, :], chosen[:, r, :, :],
                                                 scores[:, r, None, :].to_broadcast([P, q, TOPK, E]), ALU.mult), R["table"])
            R["topk_w"] = dve.do(lambda e: e.tensor_reduce(topk_w[:, r, :].rearrange("p n k -> p (n k)"),
                                                           picked[:, r, :, :].rearrange("p n k e -> p (n k) e"), AX.X,
                                                           ALU.add), m)

        def route_weights():
            m = R["topk_w"]
            m = dve.do(lambda e: e.tensor_reduce(norm[:, :], topk_w[:, :, :], AX.X, ALU.add), m)
            m = dve.do(lambda e: e.reciprocal(norm[:, :], norm[:, :]), m)
            m = dve.do(lambda e: e.tensor_tensor(topk_w[:, :, :], topk_w[:, :, :],
                                                 norm[:, :, None].to_broadcast([P, NT, TOPK]), ALU.mult), m)
            R["weights"] = dve.do(lambda e: e.tensor_scalar(topk_w[:, :, :], topk_w[:, :, :], ROUTE_SCALE / WS, None,
                                                            ALU.mult), m)

        MID = P - N

        def load_small():
            free = tuple(m for marks in stage_free for m in marks)
            gate_in = load(gate_f, gate_wt, "gate_in", *free)
            state_in = load(state_f[:, 0, :, :], state_wt, "state_in", *free)
            input_in = load(state_f[:, 1, :, :], input_wt, "input_in", *free)
            gb_in = load(bias_in[:, 0, :], gate_b_row, "gb_in", *free)
            ob_in = load(bias_in[:, 1, :], out_b_row, "ob_in", *free)
            R["small"] = (gate_in, state_in, input_in, gb_in, ob_in)

        def state_weights():
            state_in, input_in = R["small"][1:3]
            ssum = dve.do(lambda e: e.tensor_tensor(state_sum[:, :, :], state_f[:, 0, :, :], state_f[:, 1, :, :], ALU.add),
                          state_in, input_in)
            srep = dve.do(lambda e: e.tensor_copy(state_rep[:, :, :, :],
                                                  state_sum[:, :, None, :].to_broadcast([P, KD, G, N])), ssum)
            for k in range(KD):
                sw = dve.do(lambda e, k=k: e.tensor_scalar(state_w[:, k, :], state_sum[:, k, :], lnw_sb[:, k:k + 1], WS,
                                                           ALU.mult, ALU.mult), ssum, lnw_in)
            hi = dve.do(lambda e: e.tensor_copy(state_pad[:, 0, :, MID:P], state_w[:, :, :]), sw, z[4])
            R["state_w"] = dve.do(lambda e: e.tensor_tensor(state_pad[:, 1, :, MID:P], state_w[:, :, :],
                                                            state_pad[:, 0, :, MID:P], ALU.subtract), hi)
            R["state_rep"] = srep

        def state_bias_sum():
            srep = R["state_rep"]
            for k in range(KD):
                mm = pe.do(lambda e, k=k: e.matmul(SMALL[:, 0:1], state_rep[:, k, :, :].rearrange("p g n -> p (g n)"),
                                                   lnb_sb[:, k:k + 1], start=k == 0, stop=k == KD - 1), srep, lnb_in, R["experts"])
            b = dve.do(lambda e: e.tensor_tensor(state_bias[:, :], sbias[:, 0:1], sbias[:, 1:2], ALU.add), sb_in, ib_in)
            R["state_bias"] = dve.do(lambda e: e.tensor_tensor(state_bias[:, :], state_bias[:, :], SMALL[:, 0:1], ALU.add),
                                     b, mm)

        def bias_weights():
            gate_in, _, _, gb_in, ob_in = R["small"]
            for k in range(KD):
                mm = pe.do(lambda e, k=k: e.matmul(TABLE[0:1, 0:D], lnb_sb[:, k:k + 1], gate_f[:, k, :], start=k == 0,
                                                   stop=k == KD - 1), gate_in, lnb_in, R["tokens"], R["rows"])
            b0 = dve.do(lambda e: e.tensor_tensor(bias_f[:, 0, :], bias_in[:, 0, :], TABLE[0:1, 0:D], ALU.add), gb_in, mm)
            R["bias_0"] = b0
            b1 = dve.do(lambda e: e.tensor_scalar(bias_f[:, 0, :], bias_f[:, 0, :], 1.0 / DESCALE, None, ALU.mult), b0)
            last = dve.do(lambda e: e.tensor_scalar(bias_f[:, 1, :], bias_in[:, 1, :], 1.0 / DESCALE, None, ALU.mult),
                          ob_in)
            s_br = sem("bias_rows_in", 16)
            for j in range(3):
                part = dve.do(lambda e, j=j: e.tensor_copy(bias_part[:, j, :, :], bias_f[:, :, :]), b1, last)
                if j < 2:
                    last = dve.do(lambda e, j=j: e.tensor_tensor(bias_f[:, :, :], bias_f[:, :, :], bias_part[:, j, :, :],
                                                                 ALU.subtract), part)
                R["bias_rows"] = sync.do(lambda e, j=j: e.dma_start(bias_rows[j:j + 1, :, :], bias_part[:, j, :, :]), part,
                                         counter=s_br)
            R["gate_bias_product"] = mm

        def gate_weights():
            mm = R["gate_bias_product"]
            for k in range(KD):
                gw = dve.do(lambda e, k=k: e.tensor_scalar(gate_f[:, k, :], gate_f[:, k, :], lnw_sb[:, k:k + 1], WS,
                                                           ALU.mult, ALU.mult), mm, lnw_in)
            hi = dve.do(lambda e: e.tensor_copy(gate_p[:, 0, :, :], gate_f[:, :, :]), gw)
            R["gate_w"] = dve.do(lambda e: e.tensor_tensor(gate_p[:, 1, :, :], gate_f[:, :, :], gate_p[:, 0, :, :],
                                                           ALU.subtract), hi)

        U, GATE = bank[6], bank[7]
        Z = {"f": xf_free[1], "parts": (), "T": (), "gate": ()}
        gate_ready = {}

        def z_norm(b):
            ready = rstd_ready[b * BT // SB]
            for i in range(BT):
                Z["zn"] = dve.do(lambda e, n=b * BT + i, i=i: e.tensor_scalar(
                    zn_f[:, i, :], x_sb[:, n, :], mean_var[:, n, 0:1], rstd2[:, 1, n:n + 1], ALU.subtract, ALU.mult),
                    ready, *Z["f"])

        def z_hi(b):
            Z["hi"] = act.do(lambda e: e.activation(zn_parts[:, :, 0, :], zn_f[:, :, :], ACT.Copy), Z["zn"], *Z["parts"])

        def z_lo(b):
            lo = dve.do(lambda e: e.tensor_tensor(zn_parts[:, :, 1, :], zn_f[:, :, :], zn_parts[:, :, 0, :],
                                                  ALU.subtract), Z["hi"], *Z["parts"])
            Z["f"], Z["made"] = (lo,), (Z["hi"], lo)

        def z_transpose(b, part):
            t, ev = transposed(lambda j: zn_parts[:, j % BT, part, (j // BT) * P:(j // BT + 1) * P], zT[:, part, :, :],
                               (Z["made"][part],), act if part == 0 else dve, *Z["T"])
            Z["parts"] = (t,)
            Z.setdefault("ev", []).append(ev)

        def z_input(b):
            ready, Z["ev"] = tuple(Z["ev"][-2:]), []
            Z["ready"] = ready
            steps = [(k, pz, pw) for k in range(KD) for pz, pw in SPLIT3]
            for j, (k, pz, pw) in enumerate(steps):
                R["u"] = pe.do(lambda e, j=j, k=k, pz=pz, pw=pw:
                               e.matmul(U[:, :], state_pad[:, pw, k, MID - b * N:MID - b * N + P], zT[:, pz, k, :],
                                        start=b == 0 and j == 0, stop=b == NB - 1 and j == len(steps) - 1),
                               *ready, R["state_w"], R["state_bias"], quiet=j < len(steps) - 1)

        def z_gate(b, half):
            for i2 in range(2):
                i = half * 2 + i2
                steps = [(k, pz, pw) for k in range(KD) for pz, pw in SPLIT3]
                for j, (k, pz, pw) in enumerate(steps):
                    pe.do(lambda e, i=i, i2=i2, j=j, k=k, pz=pz, pw=pw:
                          e.matmul(GATE[:, i2 * D:(i2 + 1) * D], zT[:, pz, k, i * P:(i + 1) * P], gate_p[:, pw, k, :],
                                   start=j == 0, stop=False), R["gate_w"], R["bias_0"], *Z["ready"], *Z["gate"],
                          quiet=True)
                gm = pe.do(lambda e, i2=i2: e.matmul(GATE[:, i2 * D:(i2 + 1) * D], ones_row3[:, :], bias_rows[:, 0, :],
                                                     start=False, stop=True), R["bias_rows"], ones_ready[1])
            n = b * BT + half * 2
            gs = act.do(lambda e: e.activation(mix_sb[:, n:n + 2, :].rearrange("p n d -> p (n d)"), GATE[:, :],
                                               ACT.Tanh, scale=0.5 * DESCALE), gm, R["weights"])
            Z["gate"], Z["T"] = (gs,), (gm,)
            gate_ready[n] = gate_ready[n + 1] = gs

        def u_done():
            R["u_sb"] = act.do(lambda e: e.activation(u_sb[:, :, :].rearrange("p c j -> p (c j)"), U[:, :], ACT.Identity,
                                                      bias=state_bias[:, 0:1], scale=DESCALE), R["u"], R["state_bias"])

        SP = [bank[6], bank[7]]
        scan = {"tanh": None, "n": 0, "start": None, "free": None}

        def scan_step(p, j):
            if scan["free"] is None:
                scan["free"] = [(R["u_sb"],), Z["gate"]]
            n = scan["n"]
            sp, first = SP[n % 2], p == 0 and j == 0
            a = pe.do(lambda e: e.matmul(sp[:, 0:C], ident_f[:, :], u_sb[:, :, j], start=True, stop=first), idf,
                      R["u_sb"], *scan["free"][n % 2])
            if not first:
                h = H[p][:, :, j - 1] if j else start[p - 1][:, :]
                a = pe.do(lambda e: e.matmul(sp[:, 0:C], rec_bd[:, :], h, start=False, stop=True), rec_in,
                          scan["tanh"] if j else scan["start"])
            t = act.do(lambda e: e.activation(H[p][:, :, j], sp[:, 0:C], ACT.Tanh), a)
            scan["tanh"], scan["n"], scan["free"][n % 2] = t, n + 1, (t,)

        def scan_shift(p):
            n = scan["n"]
            sp = SP[n % 2]
            m = pe.do(lambda e: e.matmul(sp[:, 0:1], shift_f[:, :], H[p][:, C - 1:C, L - 1], start=True, stop=True),
                      shift_ready, scan["tanh"], *scan["free"][n % 2])
            dve.do(lambda e: e.tensor_copy(start[p][:, 1:C], H[p][:, 0:C - 1, L - 1]), scan["tanh"])
            b = dve.do(lambda e: e.tensor_copy(start[p][:, 0:1], sp[:, 0:1]), m)
            scan["n"], scan["start"], scan["free"][n % 2] = n + 1, b, (b,)

        def scan_check():
            n = scan["n"]
            sp = SP[n % 2]
            d = dve.do(lambda e: e.tensor_tensor(differ[:, :], start[0][:, :], start[1][:, :], ALU.not_equal), scan["start"])
            d = dve.do(lambda e: e.tensor_reduce(differ_max[:, :], differ[:, :], AX.X, ALU.add), d)
            m = pe.do(lambda e: e.matmul(sp[0:1, 0:1], differ_max[:, :], ones_col[:, :], start=True, stop=True), d,
                      ones_ready[0], *scan["free"][n % 2])
            R["flag"] = dve.do(lambda e: e.tensor_copy(flag[:, :], sp[0:1, 0:1]), m)

        GU, HT, YP = [bank[2], bank[3]], bank[4], bank[5]
        s_xg = [sem(f"x_gathered{i}", 16) for i in range(XG_RING)]
        s_ys = [sem(f"y_scattered{i}", 16) for i in range(YS_RING)]
        M = {"gathered": {}, "xg_read": {}, "xT": {}, "gu": {}, "gu_free": {}, "h": {}, "ht_free": (), "yp_free": (),
             "scattered": {}, "down": {}, "ys": {}, "hf": {}, "htc": {}, "hT": {}}
        expert_value = {}

        def gather(n):
            free = (M["xg_read"][n - XG_RING],) if n >= XG_RING else (shared["last"], *xp_out)
            for j in range(2):
                M["gathered"][n] = pool.do(lambda e, j=j: e.indirect_dma_start(
                    out=x_ring[:, n % XG_RING, j, :], out_offset=None, in_=x_parts_dram,
                    in_offset=bass.IndirectOffsetOnAxis(ap=token_of[:, 2 * n + j:2 * n + j + 1], axis=0)),
                    R["tokens"], *free, counter=s_xg[n % XG_RING])

        def scatter(n):
            for j in range(2):
                M["scattered"][n] = pool.do(lambda e, j=j: e.indirect_dma_start(
                    out=y_dram, out_offset=bass.IndirectOffsetOnAxis(ap=row_of[:, 2 * n + j:2 * n + j + 1], axis=0),
                    in_=y_ring[:, n % YS_RING, j, :], in_offset=None), R["rows"], M["ys"][n],
                    counter=s_ys[n % YS_RING])

        VL = 8

        def load_experts(b0):
            def make(e):
                loads, values = nc.values_load_multi_w_load_instructions(
                    expert_of[0:1, b0:b0 + VL], engines=[e.engine], min_val=0, max_val=E - 1,
                    skip_runtime_bounds_check_because="a count of at most E experts, clamped to E - 1 on the chip")
                for i, v in enumerate(values):
                    expert_value[b0 + i] = v
                return loads[-1]
            pe.do(make, R["experts"], quiet=True)

        def pair_x(n):
            s = n % 2
            free = (M["gu"][n - 2],) if n >= 2 else (shared["last"],)
            t, M["xT"][n] = transposed(lambda j: x_ring[:, n % XG_RING, j // 4, (j % 4) * P:(j % 4 + 1) * P],
                                       xg_T[:, s, :], (M["gathered"][n],), dve, *free)
            M["xg_read"][n] = t

        def pair_up(n):
            gu = GU[n % 2]
            for j in range(2):
                b = 2 * n + j
                if b % VL == 0:
                    load_experts(b)
                steps = [(k, px, pw) for k in range(KD) for px, pw in SPLIT3]
                for i, (k, px, pw) in enumerate(steps):
                    M["gu"][n] = pe.do(lambda e, b=b, j=j, i=i, k=k, px=px, pw=pw: e.matmul(
                        gu[:, j * 2 * F:(j + 1) * 2 * F],
                        xg_T[:, n % 2, ((j * 2 + px) * KD + k) * P:((j * 2 + px) * KD + k + 1) * P],
                        w_all[:, bass.ds(expert_value[b], 1), pw * WG + k * 2 * F:pw * WG + (k + 1) * 2 * F],
                        start=i == 0, stop=i == len(steps) - 1), M["xT"][n], *all_w,
                        *M["gu_free"].get(n - 2, gu_first), quiet=i < len(steps) - 1)
            gv = gu[:, :].rearrange("p (b f) -> p b f", b=2)
            sg = act.do(lambda e: e.activation(silu_sb[:, n % 2, :, :], gv[:, :, 0:F], ACT.Silu, scale=DESCALE),
                        M["gu"][n], *M["hf"].get(n - 2, ()))
            hf = dve.do(lambda e: e.scalar_tensor_tensor(out=h_sb[:, n % 2, :, :], in0=gv[:, :, F:2 * F], scalar=DESCALE,
                                                         in1=silu_sb[:, n % 2, :, :], op0=ALU.mult, op1=ALU.mult), sg,
                        *M["hf"].get(n - 2, ()))
            M["gu_free"][n] = (hf,)

        def pair_split(n):
            hf, = M["gu_free"][n]
            hh = act.do(lambda e: e.activation(h_parts[:, n % 2, :, 0, :], h_sb[:, n % 2, :, :], ACT.Copy), hf,
                        *M["htc"].get(n - 2, ()))
            hl = dve.do(lambda e: e.tensor_tensor(h_parts[:, n % 2, :, 1, :], h_sb[:, n % 2, :, :],
                                                  h_parts[:, n % 2, :, 0, :], ALU.subtract), hh)
            M["h"][n], M["hf"][n] = (hh, hl), (hl,)

        def pair_h(n):
            tb = HT[:, :].bitcast(f16)
            for q in range(4):
                t = pe.do(lambda e, q=q: e.transpose(tb[:, q * P:(q + 1) * P], h_parts[:, n % 2, q // 2, q % 2, :],
                                                     ident_h[:, :]), *M["h"][n], *M["ht_free"], quiet=q < 3)
            M["htc"][n] = (t,)
            c = dve.do(lambda e: e.tensor_copy(hT_sb[:, n % 2, :, :, :].rearrange("p b i f -> p (b i f)"), tb[:, 0:4 * P]),
                       t, *((M["down"][n - 2],) if n >= 2 else ()))
            M["ht_free"], M["hT"][n] = (c,), c

        def pair_down(n):
            for j in range(2):
                for i, (ph, pw) in enumerate(SPLIT3):
                    m = pe.do(lambda e, b=2 * n + j, j=j, i=i, ph=ph, pw=pw: e.matmul(
                        YP[:, j * D:(j + 1) * D], hT_sb[:, n % 2, j, ph, :],
                        w_all[:, bass.ds(expert_value[b], 1), 2 * WG + pw * W2:2 * WG + (pw + 1) * W2],
                        start=i == 0, stop=i == 2), M["hT"][n], *M["yp_free"], quiet=not (i == 2 and j == 1))
            M["down"][n] = m
            r = n % YS_RING
            free = (M["scattered"][n - YS_RING],) if n >= YS_RING else ()
            y = act.do(lambda e: e.activation(y_ring[:, r, :, :].rearrange("p b d -> p (b d)"), YP[:, :], ACT.Copy),
                       m, *free)
            M["yp_free"], M["ys"][n] = (y,), y

        fb = {k: ctx.enter_context(nc.semaphore(f"fb_{k}")) for k in ("sum", "state", "next", "copied", "end_act", "end_dve")}

        def differs(eng):
            flag_ready = R["flag"]
            eng.wait_ge(flag_ready[0].handle, flag_ready[1])
            return eng.value_load(flag[0:1, 0:1], min_val=0, max_val=P * C)

        def take(eng, s):
            eng.wait_ge(s, 1)
            eng.sem_inc(s, -1)

        PASSES = T // SEQS // L - 1

        def fallback_pe(eng):
            v = differs(eng)
            with eng.If(v != 0):
                with eng.Fori(0, PASSES):
                    for j in range(L):
                        eng.matmul(SP[0][:, 0:C], ident_f[:, :], u_sb[:, :, j], start=True, stop=False)
                        h = H[1][:, :, j - 1] if j else start[1][:, :]
                        eng.matmul(SP[0][:, 0:C], rec_bd[:, :], h, start=False, stop=True).then_inc(fb["sum"], 1)
                        take(eng, fb["state"])
                    eng.matmul(SP[1][:, 0:1], shift_f[:, :], H[1][:, C - 1:C, L - 1], start=True, stop=True)\
                        .then_inc(fb["next"], 1)
                    take(eng, fb["copied"])
                eng.sem_inc(fb["end_act"], 1)
                eng.sem_inc(fb["end_dve"], 1)

        def fallback_act(eng):
            v = differs(eng)
            with eng.If(v != 0):
                with eng.Fori(0, PASSES):
                    for j in range(L):
                        take(eng, fb["sum"])
                        eng.activation(H[1][:, :, j], SP[0][:, 0:C], ACT.Tanh).then_inc(fb["state"], 1)
                take(eng, fb["end_act"])

        def fallback_dve(eng):
            v = differs(eng)
            with eng.If(v != 0):
                with eng.Fori(0, PASSES):
                    take(eng, fb["next"])
                    eng.tensor_copy(start[1][:, 1:C], H[1][:, 0:C - 1, L - 1])
                    eng.tensor_copy(start[1][:, 0:1], SP[1][:, 0:1]).then_inc(fb["copied"], 1)
                take(eng, fb["end_dve"])

        def general_recurrence():
            for q, steps in ((pe, fallback_pe), (act, fallback_act), (dve, fallback_dve)):
                q.do(steps, quiet=True)

        O = {"free": [(), ()]}
        Hv = [H_p[:, i, :, :].rearrange("p c j -> p (c j)") for i in range(2)]

        def out_weights():
            outw_in = sync.do(lambda e: e.dma_start(zn_f[:, 1, :], out_wt), *Z["f"], counter=sem("outw_in", 16))
            zero = pool.do(lambda e: e.memset(outw_p[:, :, :, :], 0.0), shared["last"])
            hi = dve.do(lambda e: e.tensor_scalar(outw_c[:, 0, :], zn_f[:, 1, :], WS, None, ALU.mult), outw_in)
            lo = dve.do(lambda e: e.scalar_tensor_tensor(out=outw_c[:, 1, :], in0=zn_f[:, 1, :], scalar=WS,
                                                         in1=outw_c[:, 0, :], op0=ALU.mult, op1=ALU.subtract), hi)
            s_ow = sem("outw_placed", 16)
            for g in range(G):
                O["w"] = sync.do(lambda e, g=g: e.dma_start(outw_p[g * N:(g + 1) * N, :, g, :],
                                                            outw_c[g * N:(g + 1) * N, :, :]), lo, zero, counter=s_ow)

        def state_parts():
            hh = act.do(lambda e: e.activation(H_p[:, 0, :, :], H[1][:, :, :], ACT.Copy, scale=XS), R["flag"])
            O["h"] = (hh, dve.do(lambda e: e.scalar_tensor_tensor(out=H_p[:, 1, :, :], in0=H[1][:, :, :], scalar=XS,
                                                                  in1=H_p[:, 0, :, :], op0=ALU.mult, op1=ALU.subtract), hh))

        def out_mix(n):
            ob, g, i = SP[n % 2], n // BT, n % BT
            for j, (ph, pw) in enumerate(SPLIT3):
                pe.do(lambda e, j=j, ph=ph, pw=pw, ob=ob, g=g, i=i:
                      e.matmul(ob[:, 0:D], Hv[ph][:, i * P:(i + 1) * P], outw_p[:, pw, g, :], start=j == 0, stop=False),
                      *O["h"], O["w"], *O["free"][n % 2], quiet=True)
            om = pe.do(lambda e, ob=ob: e.matmul(ob[:, 0:D], ones_row3[:, :], bias_rows[:, 1, :], start=False, stop=True),
                       R["bias_rows"])
            q = dve.do(lambda e: e.tensor_scalar(xn_f[:, n % BT, :], x_sb[:, n, :], mean_var[:, n, 0:1],
                                                 rstd2[:, 0, n:n + 1], ALU.subtract, ALU.mult),
                       *shared["y_free"][0], *shared["y_free"][1], *O.get(("q", n - BT), ()))
            a = dve.do(lambda e: e.scalar_tensor_tensor(out=mix_sb[:, n, :], in0=mix_sb[:, n, :], scalar=1.0,
                                                        in1=ob[:, 0:D], op0=ALU.add, op1=ALU.mult), om, gate_ready[n])
            O["free"][n % 2] = (a,)
            O["mix", n] = dve.do(lambda e: e.scalar_tensor_tensor(
                out=mix_sb[:, n, :], in0=mix_sb[:, n, :], scalar=0.5 * DESCALE * XS, in1=xn_f[:, n % BT, :], op0=ALU.mult,
                op1=ALU.add), a, q)
            O["q", n] = (O["mix", n],)

        route_blocks()
        shared_down(0)
        shared_up(1)
        route_slots()
        shared_hidden(1)
        shared_down(1)
        ahead = 2
        for n in range(NT):
            table_tile(n)
            b = ahead + n // 5
            if n % 5 == 0 and b < NB:
                shared_up(b)
            if n % 5 == 3 and b < NB:
                shared_hidden(b)
            if n % 5 == 1 and ahead < b <= NB:
                shared_down(b - 1)
            if n % 3 == 0 and NB + n // 3 <= E:
                split_weights(NB + n // 3)
        finish_table()
        all_w = w_ready[E - 1]
        gu_first = (R["sc"], R["slot_e"])
        M["yp_free"], M["ht_free"] = shared["up_free"], shared["up_free"]
        tp["free"] = list(shared["free"])

        SLOTS = 3
        load_small()
        side = [(pick_weights, 0), (pick_weights, 1), (pick_weights, 2), (pick_weights, 3), None, (route_weights,),
                (z_norm, 0), (state_weights,), (z_hi, 0), (state_bias_sum,), (z_lo, 0), (bias_weights,), (z_transpose, 0, 0),
                (z_transpose, 0, 1), (gate_weights,), None]
        for b in range(NB):
            more = b + 1 < NB
            side += [(z_input, b), (z_norm, b + 1) if more else None, (z_gate, b, 0), (z_hi, b + 1) if more else None,
                     (z_gate, b, 1), (z_lo, b + 1) if more else None, None]
            side += [(z_transpose, b + 1, 0), (z_transpose, b + 1, 1), None] if more else []
        side += [(u_done,), None]
        for p in range(2):
            side += [(scan_step, p, j) for j in range(L)] + [(scan_shift, p)]
        side += [(out_weights,), (scan_check,), None, None, None, (general_recurrence,), (state_parts,), None, None]
        room = SLOTS * NPAIR - len(side)
        assert room >= NT
        for n in range(NT):
            side += [(out_mix, n)] + [None] * (room * (n + 1) // NT - room * n // NT - 1)

        def beside(slot):
            if slot < len(side) and side[slot] is not None:
                step, *args = side[slot]
                step(*args)

        AHEAD = XG_RING - 2
        for n in range(AHEAD):
            gather(n)
        pair_x(0)
        pair_x(1)
        pair_up(0)
        pair_split(0)
        for n in range(NPAIR + 1):
            if n + AHEAD < NPAIR:
                gather(n + AHEAD)
            if n >= 2:
                scatter(n - 2)
            if n + 2 < NPAIR:
                pair_x(n + 2)
            beside(SLOTS * n)
            if n + 1 < NPAIR:
                pair_up(n + 1)
                pair_split(n + 1)
            beside(SLOTS * n + 1)
            if n < NPAIR:
                pair_h(n)
            beside(SLOTS * n + 2)
            if n >= 1:
                pair_down(n - 1)
        scatter(NPAIR - 1)
        all_scattered = [M["scattered"][n] for n in range(NPAIR - YS_RING, NPAIR)]

        s_yin = [sem(f"y_in{i}", 16) for i in range(FIN_RING)]
        y_view = y_dram[0:T * TOPK, :].rearrange("(n p k) d -> p n k d", p=P, k=TOPK)

        s_out = [sem(f"out_stored{i}", 16) for i in range(FIN_RING)]
        o_view = out.rearrange("(n p) d -> p n d", p=P)
        last_pe = M["down"][NPAIR - 1]
        stored, y_in, finished = {}, {}, []

        def load_results(n):
            r = n % FIN_RING
            free = (stored[n - FIN_RING],) if n >= FIN_RING else (last_pe,)
            sync.do(lambda e: e.dma_start(fin_ring[:, r, TOPK, :], ysh_view[:, n, :]),
                    *shared["y_free"][0], *shared["y_free"][1], *free, counter=s_yin[r])
            y_in[n] = sync.do(lambda e: e.dma_start(fin_ring[:, r, 0:TOPK, :], y_view[:, n, :, :]), *all_scattered,
                              counter=s_yin[r])

        def result(n):
            r = n % FIN_RING
            acc, c = fin_ring[:, r, TOPK, :], y_in[n]
            for k in range(TOPK):
                c = dve.do(lambda e, k=k: e.scalar_tensor_tensor(
                    out=acc, in0=fin_ring[:, r, k, :], scalar=topk_w[:, n, k:k + 1], in1=acc, op0=ALU.mult, op1=ALU.add),
                    c, R["weights"])
            sg = act.do(lambda e: e.activation(acc, acc, ACT.Silu), c)
            m = pool.do(lambda e: e.tensor_tensor(acc, acc, mix_sb[:, n, :], ALU.mult), sg, O["mix", n])
            finished.append((n, acc, m))

        def store(n, acc, m):
            m = dve.do(lambda e: e.scalar_tensor_tensor(out=acc, in0=acc, scalar=1.0 / XS, in1=x_sb[:, n, :], op0=ALU.mult,
                                                        op1=ALU.add), m)
            stored[n] = act.do(lambda e: e.dma_start(o_view[:, n, :], acc), m, counter=s_out[n % FIN_RING])

        LOADS = FIN_RING - 3
        for n in range(LOADS):
            load_results(n)
        for n in range(NT):
            result(n)
            if len(finished) > 2:
                store(*finished.pop(0))
            if n + LOADS < NT:
                load_results(n + LOADS)
        for step in finished:
            store(*step)
        for n in range(NT - FIN_RING, NT):
            sync.do(lambda e: e.nop(), stored[n], quiet=True)

        block = ctx.enter_context(nc.Block())

        @block.tensor
        def _(eng):
            pe.emit(eng)

        @block.scalar
        def _(eng):
            act.emit(eng)

        @block.vector
        def _(eng):
            dve.emit(eng)

        @block.gpsimd
        def _(eng):
            pool.emit(eng)

        @block.sync
        def _(eng):
            sync.emit(eng)


def kernel(**inputs):
    import concourse.bacc as bacc
    from concourse.bass_utils import run_bass_kernel_spmd

    a = {k: np.asarray(v) for k, v in inputs.items()}
    P = 128
    B, S, D = a["L0_attn_x"].shape

    def on_partitions(w):
        return w.reshape(w.shape[0], D // P, P).transpose(2, 1, 0)

    w13 = np.concatenate([a["L0_ffn_w13"], a["L0_ffn_w13_s"][None]])
    w2 = np.concatenate([a["L0_ffn_w2"], a["L0_ffn_w2_s"][None]])
    n_e, gu, _ = w13.shape
    n = a["L0_attn_A"].shape[0]
    arrays = {
        "x": a["L0_attn_x"].reshape(B * S, D),
        "w13t": w13.reshape(n_e, gu, D // P, P).transpose(3, 0, 2, 1).reshape(P, n_e, (D // P) * gu),
        "w2t": w2.transpose(2, 0, 1),
        "router_wt": on_partitions(a["L0_ffn_gate_w"]),
        "router_b": a["L0_ffn_gate_b"][None],
        "gate_wt": on_partitions(a["L0_attn_Wg"]),
        "gate_b_row": a["L0_attn_bg"][None],
        "state_wt": on_partitions(a["L0_attn_Ws"]),
        "input_wt": on_partitions(a["L0_attn_Wi"]),
        "state_b": np.tile(a["L0_attn_bs"], P // n)[:, None],
        "input_b": np.tile(a["L0_attn_bi"], P // n)[:, None],
        "rec_at": a["L0_attn_A"].T,
        "out_wt": np.tile(a["L0_attn_Wo"].T, (P // n, 1)),
        "out_b_row": a["L0_attn_bo"][None],
        "ln_w": a["L0_attn_ln_w"].reshape(D // P, P).T,
        "ln_b": a["L0_attn_ln_b"].reshape(D // P, P).T,
    }
    arrays = {f"in_{k}": np.ascontiguousarray(v) for k, v in arrays.items()}
    nc = bacc.Bacc("TRN2", target_bir_lowering=False, num_devices=1)
    args = [nc.dram_tensor(k, v.shape, mybir.dt.from_np(v.dtype), kind="ExternalInput").ap() for k, v in arrays.items()]
    out = nc.dram_tensor("out", (B * S, D), mybir.dt.float32, kind="ExternalOutput").ap()
    tokens, topk = B * S, 4
    x_parts = nc.dram_tensor("x_parts", (tokens, 2 * D), mybir.dt.float16, kind="Internal").ap()
    routed_y = nc.dram_tensor("routed_y", (tokens * topk + (tokens * topk // P + a["L0_ffn_gate_w"].shape[0]) * P, D), mybir.dt.float32, kind="Internal").ap()
    shared_y = nc.dram_tensor("shared_y", (tokens, D), mybir.dt.float32, kind="Internal").ap()
    recurrent_gated_moe(nc, *args, out, x_parts, routed_y, shared_y)
    r = run_bass_kernel_spmd(nc, [arrays], core_ids=[0])
    return r.results[0]["out"].reshape(B, S, D)
```

```python
import concourse.bass as bass
from concourse import mybir
from contextlib import ExitStack

import numpy as np


class Counter:

    def __init__(self, handle, unit=1):
        self.handle, self.unit, self.value = handle, unit, 0

    def give(self):
        self.value += self.unit
        return self, self.value


class Queue:

    def __init__(self, counter):
        self.steps, self.counter = [], counter

    def do(self, make, *marks, counter=None, quiet=False):
        mark = None if quiet else (counter or self.counter).give()
        self.steps.append((make, marks, mark))
        return mark

    def emit(self, engine):
        reached = {}
        for make, marks, mark in self.steps:
            for sig, value in marks:
                if reached.get(sig.handle.name, 0) < value:
                    engine.wait_ge(sig.handle, value)
                    reached[sig.handle.name] = value
            instruction = make(engine)
            if mark is not None:
                instruction.then_inc(mark[0].handle, mark[0].unit)


def recurrent_gated_moe(nc: bass.Bass, x, w13t, w2t, router_wt, router_b, gate_wt, gate_b_row, state_wt, input_wt,
                        state_b, input_b, rec_at, out_wt, out_b_row, ln_w, ln_b, out, x_parts_dram, y_dram, ys_dram):
    f32, f16, bf16, i32, u32 = (mybir.dt.float32, mybir.dt.float16, mybir.dt.bfloat16, mybir.dt.int32,
                                mybir.dt.uint32)
    ALU, ACT, AX = mybir.AluOpType, mybir.ActivationFunctionType, mybir.AxisListType

    P = 128
    T, D = x.shape
    KD = D // P
    NT = T // P
    E = router_wt.shape[2]
    N = rec_at.shape[0]
    F = w2t.shape[0]
    TOPK = 4
    ROUTE_SCALE = 2.5
    EPS = 1e-5
    BT = 4
    NB = NT // BT
    BW = BT * P
    G = P // N
    L = 16
    C = BW // L
    SEQS = 2
    XS, WS = 16.0, 64.0
    DESCALE = 1.0 / (XS * WS)
    NBLK = T * TOPK // P + E
    NPAIR = NBLK // 2
    USED = (T * TOPK + E * (P - 1)) // P
    WG, W2 = KD * 2 * F, D
    WE = 2 * WG + 2 * W2
    STAGES = 4
    SPLIT3 = ((0, 0), (0, 1), (1, 0))

    ctx = ExitStack()
    with ctx:
        def sb(name, shape, dt=f32):
            return ctx.enter_context(nc.sbuf_tensor(name, shape, dt))

        def sem(name, unit=1):
            return Counter(ctx.enter_context(nc.semaphore(name)), unit)

        x_sb = sb("x_sb", [P, NT, D])
        mix_sb = sb("mix_sb", [P, NT, D])
        w_all = sb("w_all", [P, E, WE], f16)
        w_shared = sb("w_shared", [P, WE], f16)
        w_stage = sb("w_stage", [P, STAGES, WG + W2])
        xT = sb("xT", [P, 2, KD, T], f16)
        xn_f = sb("xn_f", [P, BT, D])
        xn_parts = sb("xn_parts", [P, 2, BT, 2, D], f16)
        zn_f = sb("zn_f", [P, BT, D])
        zn_parts = sb("zn_parts", [P, BT, 2, D], f16)
        zT = sb("zT", [P, 2, KD, BW], f16)
        mean_var = sb("mean_var", [P, NT, 2])
        var2 = sb("var2", [P, 2, NT])
        root2 = sb("root2", [P, 2, NT])
        xn_bias = sb("xn_bias", [P, NT])
        xn_scale = sb("xn_scale", [P, NT])
        newton = sb("newton", [P, 2, NT])
        rstd2 = sb("rstd2", [P, 2, NT])
        ident_f = sb("ident_f", [P, P])
        ident_h = sb("ident_h", [P, P], f16)
        shift_f = sb("shift_f", [P, P])
        before_h = sb("before_h", [P, P], f16)
        ones_h = sb("ones_h", [P, P], f16)
        tri_h = sb("tri_h", [E, 2, E], f16)
        ones_col = sb("ones_col", [P, 1])
        ones_row3 = sb("ones_row3", [3, P], bf16)
        lnw_sb = sb("lnw_sb", [P, KD])
        lnb_sb = sb("lnb_sb", [P, KD])
        router_f = sb("router_f", [P, KD, E])
        router_p = sb("router_p", [P, 2, KD, E], f16)
        router_bias = sb("router_bias", [P, E])
        gate_p = sb("gate_p", [P, 2, KD, D], f16)
        state_pad = sb("state_pad", [P, 2, KD, 2 * P - N], f16)
        sbias = sb("sbias", [P, 2])
        state_bias = sb("state_bias", [P, 1])
        rec_bd = sb("rec_bd", [P, P])
        bias_rows = sb("bias_rows", [3, 2, D], bf16)
        u_sb = sb("u_sb", [P, C, L])
        H = [sb(f"H{i}", [P, C, L]) for i in range(2)]
        H_p = sb("H_p", [P, 2, C, L], f16)
        start = [sb(f"start{i}", [P, C]) for i in range(2)]
        differ = sb("differ", [P, C])
        differ_max = sb("differ_max", [P, 1])
        flag = sb("flag", [1, 1], i32)
        topk_w = sb("topk_w", [P, NT, TOPK])
        token_of = sb("token_of", [P, NBLK], u32)
        row_of = sb("row_of", [P, NBLK], u32)
        expert_of = sb("expert_of", [1, NBLK], i32)
        hT_sb = sb("hT_sb", [P, 2, 2, 2, P], f16)
        h_parts = sb("h_parts", [P, 2, 2, 2, F], f16)
        iota_blk = sb("iota_blk", [P, NBLK], f16)

        scratch, at = mix_sb[:, :, :].rearrange("p n d -> p (n d)"), [0]

        def scratch_of(width, pattern=None, dt=f32, rows=P, **dims):
            v = scratch[0:rows, at[0]:at[0] + width]
            at[0] += width
            assert at[0] <= NT * D
            v = v if dt is f32 else v.bitcast(dt)
            return v.rearrange(pattern, **dims) if pattern else v

        iota_4 = scratch_of(NBLK * TOPK // 2, "p (s k) -> p s k", dt=f16, k=TOPK)
        scores = scratch_of(NT * E, "p (n e) -> p n e", e=E)
        idx_h = scratch_of(NT * TOPK // 2, "p (n k) -> p n k", dt=f16, k=TOPK)
        chosen = scratch_of(TOPK * NT * E // 2, "p (n k e) -> p n k e", dt=f16, k=TOPK, e=E)
        chosen_any = scratch_of(NT * E // 2, "p (n e) -> p n e", dt=f16, e=E)
        chosen_2 = scratch_of(2 * BT * E, "p (n k e) -> p n k e", dt=f16, n=2 * BT, k=2)
        chosen_group = scratch_of(E // 2, dt=f16)
        chosen_before = scratch_of((NB // 2 + 1) * E // 2, "p (b e) -> p b e", dt=f16, e=E)
        slot_e = scratch_of(NT * E, "p (n e) -> p n e", e=E)
        slot_f = scratch_of(NT * TOPK, "p (n k) -> p n k", k=TOPK)
        slot_i = scratch_of(NT * TOPK, dt=i32)
        part_i = scratch_of(2 * NT * TOPK, "p (i n) -> p i n", dt=i32, i=2)
        slot_lo = scratch_of(NT * TOPK // 2, "p (n k) -> p n k", dt=f16, k=TOPK)
        entry_h = scratch_of(NT * TOPK // 2, "p (n k) -> p n k", dt=f16, k=TOPK)
        slot_hi = scratch_of(NT * TOPK // 2, "p (n k) -> p n k", dt=f16, k=TOPK)
        entry = scratch_of(NT * TOPK, "p (n k) -> p n k", k=TOPK)
        norm = scratch_of(NT)
        count_i = scratch_of(2, dt=i32)
        nblk_f = scratch_of(1)
        nblk_h = scratch_of(P // 2, dt=f16)
        blk_end = scratch_of(1)
        blk_start = scratch_of(E)
        ended = scratch_of(NBLK)
        pad_row = scratch_of(NBLK)
        stats = scratch_of(NT * 6, "p (n i) -> p n i", i=6)
        empty = scratch_of(NBLK)
        rows_f = scratch_of(NBLK)
        rows_i = scratch_of(NBLK, dt=i32)
        picked_at = at[0]
        biased = scratch_of(NT * E, "p (n e) -> p n e", e=E)
        top8 = scratch_of(NT * 8, "p (n e) -> p n e", e=8)
        idx8 = scratch_of(NT * 8, "p (n e) -> p n e", dt=u32, e=8)
        at[0] = picked_at
        picked = scratch_of(NT * TOPK * E, "p (n k e) -> p n k e", k=TOPK, e=E)
        at[0] = picked_at
        HOT_RING = 5
        lo_hot = scratch_of(HOT_RING * TOPK * P // 2, "p (r s k) -> p r s k", dt=f16, r=HOT_RING, k=TOPK)
        hi_hot = scratch_of(HOT_RING * TOPK * NBLK // 2, "p (r s k) -> p r s k", dt=f16, r=HOT_RING, k=TOPK)

        stage = [w_stage[:, i, :] for i in range(STAGES)]
        stages, used = w_stage[:, :, :].rearrange("p s w -> p (s w)"), [0]

        def stage_of(width, pattern=None, **dims):
            v = stages[:, used[0]:used[0] + width]
            used[0] += width
            assert used[0] <= STAGES * (WG + W2)
            return v.rearrange(pattern, **dims) if pattern else v

        gate_f = stage_of(KD * D, "p (k d) -> p k d", k=KD)
        state_f = stage_of(2 * KD * N, "p (i k n) -> p i k n", i=2, k=KD)
        state_rep = stage_of(KD * G * N, "p (k g n) -> p k g n", k=KD, g=G)
        state_sum = stage_of(KD * N, "p (k n) -> p k n", k=KD)
        state_w = stage_of(KD * N, "p (k n) -> p k n", k=KD)
        bias_in = stage_of(2 * D, "p (b d) -> p b d", b=2)[0:1]
        bias_f = stage_of(2 * D, "p (b d) -> p b d", b=2)[0:1]
        bias_part = stage_of(3 * D)[0:1].bitcast(bf16).rearrange("p (j b d) -> p j b d", j=3, b=2)

        sh_silu = xn_parts[:, 0, 0:2, :, :].rearrange("p b i d -> p (b i d)").bitcast(f32)
        sh_h = xn_parts[:, 0, 2:4, :, :].rearrange("p b i d -> p (b i d)").bitcast(f32)
        sh_parts = xn_parts[:, 1, 0:2, :, :].rearrange("p b i d -> p b (i d)")
        sh_y = xn_f[:, :, :].rearrange("p (s b) d -> p s b d", s=2)
        PW = 2 * 2 * D
        xg_T = xn_parts[:, 0, :, :, :].rearrange("p b i d -> p (b i d)").rearrange("p (s w) -> p s w", w=PW)
        silu_sb = xn_parts[:, 1, 0:2, :, :].rearrange("p b i d -> p (b i d)").bitcast(f32)\
            .rearrange("p (s b f) -> p s b f", s=2, b=2)
        h_sb = xn_parts[:, 1, 2:4, :, :].rearrange("p b i d -> p (b i d)").bitcast(f32)\
            .rearrange("p (s b f) -> p s b f", s=2, b=2)
        XG_RING, YS_RING = 7, 5
        xT_flat = xT[:, :, :, :].rearrange("p i k t -> p (i k t)")
        x_ring = xT_flat[:, 0:XG_RING * PW].rearrange("p (r b w) -> p r b w", r=XG_RING, b=2)
        y_at = XG_RING * PW
        y_ring = xT_flat[:, y_at:y_at + YS_RING * 4 * D].bitcast(f32).rearrange("p (r b d) -> p r b d", r=YS_RING, b=2)
        o_at = y_at + YS_RING * 4 * D
        outw_p = xT_flat[:, o_at:o_at + 2 * G * D].rearrange("p (i g d) -> p i g d", i=2, g=G)
        outw_c = zn_f[:, 0, :].bitcast(f16).rearrange("p (i d) -> p i d", i=2)
        FIN_RING, FT = 4, 2
        w_flat = w_all[:, :, :].rearrange("p e w -> p (e w)")
        fin_size = 2 * FIN_RING * FT * TOPK * D
        fin_y = w_flat[:, 0:fin_size].bitcast(f32).rearrange("p (r n k d) -> p r n k d", r=FIN_RING, n=FT, k=TOPK)
        fin_sum = w_flat[:, fin_size:fin_size + fin_size // TOPK].bitcast(f32)\
            .rearrange("p (r n d) -> p r n d", r=FIN_RING, n=FT)

        bank = [ctx.enter_context(nc.psum_tensor(f"bank{i}", [P, 512], f32)) for i in range(8)]

        s_pe, s_act, s_dve, s_pool = sem("pe_done"), sem("act_done"), sem("dve_done"), sem("pool_done")
        pe, act, dve, pool, sync = Queue(s_pe), Queue(s_act), Queue(s_dve), Queue(s_pool), Queue(None)

        def load(dst, src, name, *marks, queue=None):
            return (queue or sync).do(lambda e: e.dma_start(dst, src), *marks, counter=sem(name, 16))

        XL = 4
        x_view = x.rearrange("(n p) d -> p n d", p=P)
        x_in = [load(x_sb[:, n:n + XL, :], x_view[:, n:n + XL, :], f"x_in{n}") for n in range(0, NT, XL)]
        router_in = load(router_f[:, :, :], router_wt, "router_in", queue=act)
        rb_in = load(router_bias[:, :], router_b.broadcast_to([P, E]), "rb_in", queue=act)
        lnw_in = load(lnw_sb[:, :], ln_w, "lnw_in", queue=act)
        lnb_in = load(lnb_sb[:, :], ln_b, "lnb_in", queue=act)
        sb_in = load(sbias[:, 0:1], state_b, "sb_in", queue=act)
        ib_in = load(sbias[:, 1:2], input_b, "ib_in", queue=act)

        def diagonal(t, fill_base, zeroed, width=P):
            return pool.do(lambda e: e.affine_select(out=t, in_=t, compare_op=ALU.not_equal, fill=1.0, base=fill_base,
                                                     pattern=[[-1, width]], channel_multiplier=1), zeroed)

        z = [pool.do(lambda e, t=t: e.memset(t, 0.0)) for t in
             (ident_h[:, :], ident_f[:, :], shift_f[:, :], rec_bd[:, :], state_pad[:, :, :, :])]
        idh = diagonal(ident_h[:, :], 0, z[0])
        idf = diagonal(ident_f[:, :], 0, z[1])
        sh0 = diagonal(shift_f[:, :], N, z[2])
        shift_ready = pool.do(lambda e: e.memset(shift_f[:, P // SEQS:P // SEQS + N], 0.0), sh0)
        ones_ready = [pool.do(lambda e, t=t: e.memset(t, 1.0)) for t in
                      (ones_col[:, :], ones_row3[:, :], ones_h[:, :], before_h[:, :], tri_h[:, :, :])]
        before_ready = pool.do(lambda e: e.affine_select(out=before_h[:, :], in_=before_h[:, :], compare_op=ALU.is_gt,
                                                         fill=0.0, base=0, pattern=[[1, P]], channel_multiplier=-1),
                               ones_ready[3])
        for j, cmp in enumerate((ALU.is_ge, ALU.is_gt)):
            tri_ready = pool.do(lambda e, j=j, cmp=cmp: e.affine_select(
                out=tri_h[:, j, :], in_=tri_h[:, j, :], compare_op=cmp, fill=0.0, base=0, pattern=[[1, E]],
                channel_multiplier=-1), ones_ready[4])
        iota_e = iota_blk[:, 0:E]
        ROW_SHIFT, ROW_BASE = 13, 127 << 10

        def iota(t, pattern, base, step):
            return pool.do(lambda e: e.iota(t, pattern=pattern, base=base, channel_multiplier=step,
                                            allow_small_or_imprecise_dtypes=True))

        iotas = [iota(iota_4[:, :, :], [[1, NBLK], [0, TOPK]], 0, 0), iota(iota_blk[:, :], [[1, NBLK]], 0, 0),
                 iota(entry[:, :, :].bitcast(i32), [[P * TOPK, NT], [1, TOPK]], ROW_BASE, TOPK),
                 iota(pad_row[:, :], [[P, NBLK]], T * TOPK + ROW_BASE, 1)]
        s_bd = sem("rec_in", 16)
        for g in range(G):
            rec_in = sync.do(lambda e, g=g: e.dma_start(rec_bd[g * N:(g + 1) * N, g * N:(g + 1) * N], rec_at), z[3],
                             counter=s_bd)

        r_hi = dve.do(lambda e: e.tensor_scalar(router_p[:, 0, :, :], router_f[:, :, :], WS, None, ALU.mult), router_in)
        r_lo = dve.do(lambda e: e.scalar_tensor_tensor(out=router_p[:, 1, :, :], in0=router_f[:, :, :], scalar=WS,
                                                       in1=router_p[:, 0, :, :], op0=ALU.mult, op1=ALU.subtract), r_hi)

        stage_free, w_ready, staged = [()] * STAGES, {}, {}
        s_w13 = [sem(f"w13_in{i}", 16) for i in range(STAGES)]
        s_w2 = [sem(f"w2_in{i}", 16) for i in range(STAGES)]
        ORDER_E = (E, *range(E))

        def load_weights(n):
            e_idx, i = ORDER_E[n], n % STAGES
            staged[n] = (
                sync.do(lambda q: q.dma_start(stage[i][:, 0:WG], w13t[:, e_idx, :]), *stage_free[i], counter=s_w13[i]),
                sync.do(lambda q: q.dma_start(stage[i][:, WG:WG + W2], w2t[:, e_idx, :]), *stage_free[i], counter=s_w2[i]))

        def split_weights(n):
            e_idx, st = ORDER_E[n], stage[n % STAGES]
            dst = w_shared[:, :] if e_idx == E else w_all[:, e_idx, :]
            marks = []
            for hi, lo, src in ((dst[:, 0:WG], dst[:, WG:2 * WG], st[:, 0:WG]),
                                (dst[:, 2 * WG:2 * WG + W2], dst[:, 2 * WG + W2:WE], st[:, WG:WG + W2])):
                w = act.do(lambda q, src=src: q.activation(src, src, ACT.Copy, scale=WS), *staged[n])
                h = act.do(lambda q, hi=hi, src=src: q.activation(hi, src, ACT.Copy), w)
                marks.append(pool.do(lambda q, hi=hi, lo=lo, src=src: q.tensor_tensor(lo, src, hi, ALU.subtract), h))
            stage_free[n % STAGES], w_ready[e_idx] = (marks[1],), (h, marks[1])
            if n + STAGES <= E:
                load_weights(n + STAGES)

        for n in range(STAGES):
            load_weights(n)

        SB = NT // 4
        rstd_ready, stats_of = [], {}

        def norm_stats(q):
            r = slice(q * SB, (q + 1) * SB)
            for n in range(q * SB, (q + 1) * SB):
                st = dve.do(lambda e, n=n: e.bn_stats(stats[:, n, :], x_sb[:, n, :]), x_in[n // XL])
            for n in range(q * SB, (q + 1) * SB):
                mv = dve.do(lambda e, n=n: e.bn_aggr(mean_var[:, n, :], stats[:, n, :]), st)
            v = mean_var[:, r, 1]
            a = dve.do(lambda e: e.tensor_scalar(var2[:, 0, r], v, 1.0, EPS, ALU.mult, ALU.add), mv)
            b = dve.do(lambda e: e.tensor_scalar(var2[:, 1, r], v, 1.0 + EPS, EPS * EPS, ALU.mult, ALU.add), mv)
            stats_of[q] = act.do(lambda e: e.activation(root2[:, :, r], var2[:, :, r], ACT.Sqrt), a, b)

        def norm_scale(q):
            r = slice(q * SB, (q + 1) * SB)
            y = dve.do(lambda e: e.reciprocal(rstd2[:, :, r], root2[:, :, r]), stats_of[q])
            y = dve.do(lambda e: e.tensor_tensor(newton[:, :, r], rstd2[:, :, r], rstd2[:, :, r], ALU.mult), y)
            y = dve.do(lambda e: e.tensor_tensor(newton[:, :, r], newton[:, :, r], var2[:, :, r], ALU.mult), y)
            y = dve.do(lambda e: e.tensor_scalar(newton[:, :, r], newton[:, :, r], -0.5 * XS, 1.5 * XS, ALU.mult, ALU.add), y)
            rstd_ready.append(dve.do(lambda e: e.tensor_tensor(rstd2[:, :, r], rstd2[:, :, r], newton[:, :, r], ALU.mult), y))

        TP = [bank[0], bank[1]]
        tp = {"n": 0, "free": [(), ()]}

        def transposed(src_of, dst, ready, engine, *extra):
            s = tp["n"] % 2
            tb = TP[s][:, :].bitcast(f16)
            for j in range(2 * BT):
                t = pe.do(lambda e, j=j: e.transpose(tb[:, j * P:(j + 1) * P], src_of(j), ident_h[:, :]),
                          idh, *ready, *tp["free"][s], quiet=j < 2 * BT - 1)
            view = tb.rearrange("p (k t) -> p k t", k=KD) if len(dst.shape) == 3 else tb
            copy = (lambda e: e.activation(dst, view, ACT.Copy)) if engine is act else (lambda e: e.tensor_copy(dst, view))
            ev = engine.do(copy, t, *extra)
            tp["free"][s], tp["n"] = (ev,), tp["n"] + 1
            return t, ev

        ROUTE = [bank[2], bank[7]]
        parts_free, xf_free, xT_ready, xp_out, xn_made, xn_done = [(), ()], [(), ()], {}, [], {}, {}
        s_xp = [sem(f"x_parts_out{i}", 16) for i in range(2)]
        xp_view = x_parts_dram.rearrange("(n p) (i d) -> p n i d", p=P, i=2)

        def x_norm(b):
            ready, s = rstd_ready[b * BT // SB], b % 2
            xf = (xn_f, zn_f)[s]
            for i in range(BT):
                xn_done[b] = dve.do(lambda e, n=b * BT + i, i=i: e.tensor_scalar(xf[:, i, :], x_sb[:, n, :], mean_var[:, n, 0:1],
                                                                         rstd2[:, 0, n:n + 1], ALU.subtract, ALU.mult),
                            ready, *xf_free[s])

        def x_split(b):
            s = b % 2
            xf = (xn_f, zn_f)[s]
            xh = act.do(lambda e: e.activation(xn_parts[:, s, :, 0, :], xf[:, :, :], ACT.Copy), xn_done[b], *parts_free[s])
            xl = pool.do(lambda e: e.tensor_tensor(xn_parts[:, s, :, 1, :], xf[:, :, :], xn_parts[:, s, :, 0, :],
                                                   ALU.subtract), xh, *parts_free[s])
            xf_free[s], xn_made[b] = (xl,), (xh, xl)
            xp_out.append(sync.do(lambda e: e.dma_start(xp_view[:, b * BT:(b + 1) * BT, :, :], xn_parts[:, s, :, :, :]), xl,
                                  counter=s_xp[s]))

        def x_transpose(b):
            s, made = b % 2, []
            for part in range(2):
                t, ev = transposed(lambda j, part=part: xn_parts[:, s, j % BT, part, (j // BT) * P:(j // BT + 1) * P],
                                   xT[:, part, :, b * BW:(b + 1) * BW], (xn_made[b][part],), dve if part else act)
                made.append(ev)
            parts_free[s] = (t, xp_out[b])
            xT_ready[b] = tuple(made)

        R, RANK = {"scored": {}}, bank[3]

        def route_batch(b):
            cols = slice(b * BT * E, (b + 1) * BT * E)
            order = [(pa, pw, k) for k in range(KD) for pa in range(2) for pw in range(2)]
            for n in range(b * BT, (b + 1) * BT):
                for j, (pa, pw, k) in enumerate(order):
                    rt = pe.do(lambda e, n=n, j=j, pa=pa, pw=pw, k=k:
                               e.matmul(ROUTE[b % 2][:, n * E:(n + 1) * E], xT[:, pa, k, n * P:(n + 1) * P],
                                        router_p[:, pw, k, :], start=j == 0, stop=j == len(order) - 1),
                               *xT_ready[b], r_lo, *R["scored"].get(b - 2, ()), quiet=j < len(order) - 1)
            R["sc"] = act.do(lambda e: e.activation(scores[:, :, :].rearrange("p n e -> p (n e)")[:, cols], ROUTE[b % 2][:, cols],
                                                    ACT.Sigmoid, scale=DESCALE), rt)
            R["scored"][b] = (R["sc"],)

        GT = 2 * BT
        NG = NT // GT

        def choose(g):
            r, first = slice(g * GT, (g + 1) * GT), g * GT
            bi = dve.do(lambda e: e.tensor_tensor(biased[:, r, :], scores[:, r, :],
                                                  router_bias[:, None, :].to_broadcast([P, GT, E]), ALU.add),
                        *R["scored"][2 * g + 1], rb_in)
            for n in range(first, first + GT):
                mx = dve.do(lambda e, n=n: e.max(top8[:, n, :], biased[:, n, :]), bi)
            for n in range(first, first + GT):
                ix = dve.do(lambda e, n=n: e.max_index(idx8[:, n, :], top8[:, n, :], biased[:, n, :]), mx)
            m = dve.do(lambda e: e.tensor_copy(idx_h[:, r, :], idx8[:, r, 0:TOPK]), ix)
            m = dve.do(lambda e: e.tensor_tensor(
                chosen[:, r, :, :].rearrange("p n k e -> p (n k) e"),
                idx_h[:, r, :].rearrange("p n k -> p (n k)")[:, :, None].to_broadcast([P, GT * TOPK, E]),
                iota_e[:, None, :].to_broadcast([P, GT * TOPK, E]), ALU.is_equal), m, iotas[1])

            def add(out_, a, c, *marks):
                return dve.do(lambda e: e.tensor_tensor(out_, a, c, ALU.add), *marks)

            m = add(chosen_2[:, :, :, :], chosen[:, r, 0:2, :], chosen[:, r, 2:4, :], m)
            any_ = add(chosen_any[:, r, :], chosen_2[:, :, 0, :], chosen_2[:, :, 1, :], m)
            m = add(chosen_2[:, 0:4, 0, :], chosen_any[:, first:first + 4, :], chosen_any[:, first + 4:first + 8, :], any_)
            m = add(chosen_2[:, 0:2, 1, :], chosen_2[:, 0:2, 0, :], chosen_2[:, 2:4, 0, :], m)
            m = add(chosen_group if g else chosen_before[:, 1, :], chosen_2[:, 0, 1, :], chosen_2[:, 1, 1, :], m)
            if g:
                m = add(chosen_before[:, g + 1, :], chosen_before[:, g, :], chosen_group, m)
            R["before", g + 1], R["any", g] = m, any_

        def rank(g):
            first = g * GT
            out_of = RANK[:, first * E:(first + GT) * E]
            pe.do(lambda e: e.matmul(out_of, before_h[:, :], chosen_any[:, first:first + GT, :].rearrange("p n e -> p (n e)"),
                                     start=True, stop=False), R["any", g], before_ready, quiet=True)
            if g:
                pe.do(lambda e: e.matmul(out_of.rearrange("p (t e) -> p t e", e=E), ones_h[:, :],
                                         chosen_before[:, g:g + 1, :].to_broadcast([P, GT, E]), start=False, stop=False),
                      R["before", g], ones_ready[2], quiet=True)
            for i in range(GT - 1):
                R["rank"] = pe.do(lambda e, i=i: e.matmul(
                    RANK[:, (first + i + 1) * E:(first + GT) * E].rearrange("p (t e) -> p t e", e=E), ones_h[:, :],
                    chosen_any[:, first + i:first + i + 1, :].to_broadcast([P, GT - 1 - i, E]), start=False,
                    stop=i == GT - 2), ones_ready[2], quiet=i < GT - 2)

        SG, SU, SY = bank[4], bank[5], [bank[0], bank[1]]
        shared = {"free": [(), ()], "up_free": (), "parts_read": (), "h": (), "y_free": [(), ()], "out": []}
        s_sy = [sem(f"shared_y_out{i}", 16) for i in range(2)]
        ysh_view = ys_dram.rearrange("(n p) d -> p n d", p=P)

        def shared_up(b):
            for half, bk in ((0, SG), (1, SU)):
                steps = [(k, px, pw) for k in range(KD) for px, pw in SPLIT3]
                for j, (k, px, pw) in enumerate(steps):
                    m = pe.do(lambda e, half=half, bk=bk, j=j, k=k, px=px, pw=pw:
                              e.matmul(bk[:, :], w_shared[:, pw * WG + (2 * k + half) * F:pw * WG + (2 * k + half + 1) * F],
                                       xT[:, px, k, b * BW:(b + 1) * BW], start=j == 0, stop=j == len(steps) - 1),
                              *w_ready[E], *xT_ready[b], *shared["up_free"], quiet=j < len(steps) - 1)
                if half == 0:
                    sg = act.do(lambda e: e.activation(sh_silu, SG[:, :], ACT.Silu, scale=DESCALE), m, *shared["up_free"], *xp_out[-2:])
            shared["up"] = (m, sg)

        def shared_hidden(b):
            m, sg = shared["up"]
            hf = dve.do(lambda e: e.scalar_tensor_tensor(out=sh_h, in0=SU[:, :], scalar=DESCALE, in1=sh_silu,
                                                         op0=ALU.mult, op1=ALU.mult), m, sg, *shared["h"])
            shared["up_free"] = (hf,)
            hh = act.do(lambda e: e.activation(sh_parts[:, 0, :], sh_h, ACT.Copy), hf, *shared["parts_read"])
            shared["h"] = (hh, pool.do(lambda e: e.tensor_tensor(sh_parts[:, 1, :], sh_h, sh_parts[:, 0, :], ALU.subtract),
                                       hh))

        def shared_down(b):
            for half, bk in enumerate(SY):
                for i2 in range(2):
                    i = half * 2 + i2
                    for j, (ph, pw) in enumerate(SPLIT3):
                        m = pe.do(lambda e, i=i, i2=i2, j=j, ph=ph, pw=pw, bk=bk:
                                  e.matmul(bk[:, i2 * D:(i2 + 1) * D], sh_parts[:, ph, i * P:(i + 1) * P],
                                           w_shared[:, 2 * WG + pw * W2:2 * WG + (pw + 1) * W2], start=j == 0,
                                           stop=j == 2), *shared["h"], *tp["free"][0], *tp["free"][1],
                                  *shared["free"][half], quiet=not (i2 == 1 and j == 2))
                ev = act.do(lambda e, half=half, bk=bk: e.activation(sh_y[:, half, :, :],
                                                                     bk[:, :].rearrange("p (b d) -> p b d", b=2),
                                                                     ACT.Copy, scale=1.0 / WS), m,
                            *shared["y_free"][half], *xf_free[0])
                o = sync.do(lambda e, half=half: e.dma_start(ysh_view[:, b * BT + half * 2:b * BT + half * 2 + 2, :],
                                                             sh_y[:, half, :, :]), ev, counter=s_sy[half])
                shared["y_free"][half] = (o,)
                shared["free"][half] = (ev,)
            shared["last"], shared["parts_read"] = m, (m,)

        norm_stats(0)
        entry_ready = dve.do(lambda e: e.tensor_scalar(entry[:, :, :].bitcast(i32), entry[:, :, :].bitcast(i32), ROW_SHIFT,
                                                       None, ALU.logical_shift_left), iotas[2])
        entry_ready = dve.do(lambda e: e.tensor_copy(entry_h[:, :, :], entry[:, :, :]), entry_ready)
        norm_stats(1)
        norm_scale(0)
        for b in range(NB + 3):
            if b < NB:
                x_norm(b)
            if b < 2:
                norm_stats(b + 2)
            if b < 3:
                norm_scale(b + 1)
            if 0 <= b - 2 < NB:
                x_transpose(b - 2)
            if b < NB:
                x_split(b)
            if 0 <= b - 3 < NB:
                route_batch(b - 3)
            if b < NB:
                split_weights(b)
            if b >= 6 and b % 2 == 0:
                rank((b - 6) // 2)
            if b == NB + 2:
                shared_up(0)
            if b >= 5 and b % 2:
                choose((b - 5) // 2)
        choose(NG - 1)
        shared_hidden(0)
        rank(NG - 1)

        SMALL, TABLE = bank[6], bank[7]

        def route_blocks():
            c = pe.do(lambda e: e.matmul(SMALL[0:E, 0:1], chosen_before[:, NG, :], ones_h[:, 0:1], start=True, stop=True),
                      R["before", NG])
            m = dve.do(lambda e: e.tensor_scalar(count_i[0:E, 0:1], SMALL[0:E, 0:1], float(P - 1), None, ALU.add), c)
            m = dve.do(lambda e: e.tensor_scalar(count_i[0:E, 1:2], count_i[0:E, 0:1], 7, None,
                                                 ALU.arith_shift_right), m)
            m = dve.do(lambda e: e.tensor_copy(nblk_f[0:E, :], count_i[0:E, 1:2]), m)
            nb = dve.do(lambda e: e.tensor_copy(nblk_h[0:E, :], nblk_f[0:E, 0:1].to_broadcast([E, P])), m)
            pe.do(lambda e: e.matmul(SMALL[:, 32:32 + E], nblk_h[0:E, :], tri_h[:, 1, :], start=True, stop=True), nb,
                  tri_ready, quiet=True)
            be = pe.do(lambda e: e.matmul(SMALL[0:E, 64:65], tri_h[:, 0, :], nblk_h[0:E, 0:1], start=True, stop=True))
            bs = dve.do(lambda e: e.tensor_copy(blk_start[:, :], SMALL[:, 32:32 + E]), be)
            be = dve.do(lambda e: e.tensor_copy(blk_end[0:E, :], SMALL[0:E, 64:65]), be)
            R["slot_e"] = dve.do(lambda e: e.scalar_tensor_tensor(
                out=slot_e[:, :, :], in0=blk_start[:, None, :].to_broadcast([P, NT, E]), scalar=float(P),
                in1=RANK[:, :].rearrange("p (n e) -> p n e", e=E), op0=ALU.mult, op1=ALU.add), bs, R["rank"])
            d = dve.do(lambda e: e.tensor_scalar(ended[0:E, :], iota_blk[0:E, :], blk_end[0:E, 0:1], None, ALU.is_ge), be)
            R["eb"] = pe.do(lambda e: e.matmul(SMALL[0:1, 128:128 + NBLK], ones_col[0:E, :], ended[0:E, :], start=True,
                                               stop=True), d, ones_ready[0])

        def pick(dst, src, ready):
            m = dve.do(lambda e: e.tensor_tensor(picked[:, :, :, :], chosen[:, :, :, :],
                                                 src[:, :, None, :].to_broadcast([P, NT, TOPK, E]), ALU.mult), ready)
            return dve.do(lambda e: e.tensor_reduce(dst[:, :, :].rearrange("p n k -> p (n k)"),
                                                    picked[:, :, :, :].rearrange("p n k e -> p (n k) e"), AX.X, ALU.add), m)

        def route_slots():
            m = pick(slot_f, slot_e[:, :, :], R["slot_e"])
            m = dve.do(lambda e: e.tensor_copy(slot_i, slot_f[:, :, :].rearrange("p n k -> p (n k)")), m)
            a = dve.do(lambda e: e.tensor_scalar(part_i[:, 0, :], slot_i, P - 1, None, ALU.bitwise_and), m)
            b = dve.do(lambda e: e.tensor_scalar(part_i[:, 1, :], slot_i, 7, None, ALU.arith_shift_right), m)
            dve.do(lambda e: e.tensor_copy(slot_lo[:, :, :].rearrange("p n k -> p (n k)"), part_i[:, 0, :]), a)
            R["slots"] = dve.do(lambda e: e.tensor_copy(slot_hi[:, :, :].rearrange("p n k -> p (n k)"), part_i[:, 1, :]), b)

        hot_free = [()] * HOT_RING

        def table_tile(n):
            r = n % HOT_RING

            def each(src, width):
                return src[:, n, None, :].to_broadcast([P, width, TOPK])

            hi = dve.do(lambda e: e.tensor_tensor(hi_hot[:, r, :, :], iota_4[:, :, :], each(slot_hi, NBLK), ALU.is_equal),
                        R["slots"], iotas[0], *hot_free[r])
            lo = dve.do(lambda e: e.tensor_tensor(lo_hot[:, r, :, :], iota_4[:, 0:P, :], each(slot_lo, P), ALU.is_equal),
                        R["slots"], *hot_free[r])
            R["hot", n] = (hi, lo)

        def table_product(n):
            r, (hi, lo) = n % HOT_RING, R["hot", n]
            lo = dve.do(lambda e: e.tensor_tensor(lo_hot[:, r, :, :], lo_hot[:, r, :, :],
                                                  entry_h[:, n, None, :].to_broadcast([P, P, TOPK]), ALU.mult), lo,
                        entry_ready)
            for k in range(TOPK):
                m = pe.do(lambda e, k=k: e.matmul(TABLE[:, 0:NBLK], lo_hot[:, r, :, k], hi_hot[:, r, :, k],
                                                  start=n == 0 and k == 0, stop=n == NT - 1 and k == TOPK - 1),
                          hi, lo, quiet=k < TOPK - 1)
            hot_free[r] = (m,)
            R["table"] = m

        def finish_table():
            m = dve.do(lambda e: e.tensor_copy(rows_f[:, :], TABLE[:, 0:NBLK]), R["table"])
            a = dve.do(lambda e: e.scalar_tensor_tensor(out=empty[:, :], in0=rows_f[:, :], scalar=0.0, in1=pad_row[:, :],
                                                        op0=ALU.is_equal, op1=ALU.mult), m, iotas[3])
            m = dve.do(lambda e: e.tensor_scalar(rows_i[:, :], rows_f[:, :].bitcast(i32), ROW_SHIFT, None,
                                                 ALU.logical_shift_right), m)
            m = dve.do(lambda e: e.tensor_tensor(rows_f[:, :], empty[:, :], rows_i[:, :], ALU.add), m, a)
            R["rows"] = dve.do(lambda e: e.tensor_scalar(row_of[:, :], rows_f[:, :], -float(ROW_BASE), None, ALU.add), m)
            m = dve.do(lambda e: e.tensor_scalar(rows_i[:, :], rows_f[:, :], -float(ROW_BASE), float(T * TOPK - 1), ALU.add,
                                                 ALU.min), m)
            R["tokens"] = dve.do(lambda e: e.tensor_scalar(token_of[:, :].bitcast(i32), rows_i[:, :], 2, None,
                                                           ALU.arith_shift_right), m)
            R["experts"] = dve.do(lambda e: e.tensor_scalar(expert_of[:, :], SMALL[0:1, 128:128 + NBLK], float(E - 1),
                                                            None, ALU.min), R["eb"])

        def pick_weights(i):
            q = NT // 4
            r = slice(i * q, (i + 1) * q)
            m = dve.do(lambda e: e.tensor_tensor(picked[:, r, :, :], chosen[:, r, :, :],
                                                 scores[:, r, None, :].to_broadcast([P, q, TOPK, E]), ALU.mult), R["table"])
            R["topk_w"] = dve.do(lambda e: e.tensor_reduce(topk_w[:, r, :].rearrange("p n k -> p (n k)"),
                                                           picked[:, r, :, :].rearrange("p n k e -> p (n k) e"), AX.X,
                                                           ALU.add), m)

        def route_weights():
            m = R["topk_w"]
            m = dve.do(lambda e: e.tensor_reduce(norm[:, :], topk_w[:, :, :], AX.X, ALU.add), m)
            m = dve.do(lambda e: e.reciprocal(norm[:, :], norm[:, :]), m)
            m = dve.do(lambda e: e.tensor_tensor(topk_w[:, :, :], topk_w[:, :, :],
                                                 norm[:, :, None].to_broadcast([P, NT, TOPK]), ALU.mult), m)
            R["weights"] = dve.do(lambda e: e.tensor_scalar(topk_w[:, :, :], topk_w[:, :, :], ROUTE_SCALE / WS, None,
                                                            ALU.mult), m)

        MID = P - N

        def load_small():
            free = tuple(m for marks in stage_free for m in marks)
            gate_in = load(gate_f, gate_wt, "gate_in", *free)
            state_in = load(state_f[:, 0, :, :], state_wt, "state_in", *free)
            input_in = load(state_f[:, 1, :, :], input_wt, "input_in", *free)
            gb_in = load(bias_in[:, 0, :], gate_b_row, "gb_in", *free)
            ob_in = load(bias_in[:, 1, :], out_b_row, "ob_in", *free)
            R["small"] = (gate_in, state_in, input_in, gb_in, ob_in)

        def state_weights():
            state_in, input_in = R["small"][1:3]
            ssum = dve.do(lambda e: e.tensor_tensor(state_sum[:, :, :], state_f[:, 0, :, :], state_f[:, 1, :, :], ALU.add),
                          state_in, input_in)
            srep = dve.do(lambda e: e.tensor_copy(state_rep[:, :, :, :],
                                                  state_sum[:, :, None, :].to_broadcast([P, KD, G, N])), ssum)
            for k in range(KD):
                sw = dve.do(lambda e, k=k: e.tensor_scalar(state_w[:, k, :], state_sum[:, k, :], lnw_sb[:, k:k + 1], WS,
                                                           ALU.mult, ALU.mult), ssum, lnw_in)
            hi = dve.do(lambda e: e.tensor_copy(state_pad[:, 0, :, MID:P], state_w[:, :, :]), sw, z[4])
            R["state_w"] = dve.do(lambda e: e.tensor_tensor(state_pad[:, 1, :, MID:P], state_w[:, :, :],
                                                            state_pad[:, 0, :, MID:P], ALU.subtract), hi)
            R["state_rep"] = srep

        def state_bias_sum():
            srep = R["state_rep"]
            for k in range(KD):
                mm = pe.do(lambda e, k=k: e.matmul(SMALL[:, 0:1], state_rep[:, k, :, :].rearrange("p g n -> p (g n)"),
                                                   lnb_sb[:, k:k + 1], start=k == 0, stop=k == KD - 1), srep, lnb_in, R["experts"])
            b = dve.do(lambda e: e.tensor_tensor(state_bias[:, :], sbias[:, 0:1], sbias[:, 1:2], ALU.add), sb_in, ib_in)
            R["state_bias"] = dve.do(lambda e: e.tensor_tensor(state_bias[:, :], state_bias[:, :], SMALL[:, 0:1], ALU.add),
                                     b, mm)

        def bias_weights():
            gate_in, _, _, gb_in, ob_in = R["small"]
            for k in range(KD):
                mm = pe.do(lambda e, k=k: e.matmul(TABLE[0:1, 0:D], lnb_sb[:, k:k + 1], gate_f[:, k, :], start=k == 0,
                                                   stop=k == KD - 1), gate_in, lnb_in, R["tokens"], R["rows"])
            b0 = dve.do(lambda e: e.tensor_tensor(bias_f[:, 0, :], bias_in[:, 0, :], TABLE[0:1, 0:D], ALU.add), gb_in, mm)
            R["bias_0"] = b0
            b1 = dve.do(lambda e: e.tensor_scalar(bias_f[:, 0, :], bias_f[:, 0, :], 1.0 / DESCALE, None, ALU.mult), b0)
            last = dve.do(lambda e: e.tensor_scalar(bias_f[:, 1, :], bias_in[:, 1, :], 1.0 / DESCALE, None, ALU.mult),
                          ob_in)
            s_br = sem("bias_rows_in", 16)
            for j in range(3):
                part = dve.do(lambda e, j=j: e.tensor_copy(bias_part[:, j, :, :], bias_f[:, :, :]), b1, last)
                if j < 2:
                    last = dve.do(lambda e, j=j: e.tensor_tensor(bias_f[:, :, :], bias_f[:, :, :], bias_part[:, j, :, :],
                                                                 ALU.subtract), part)
                R["bias_rows"] = sync.do(lambda e, j=j: e.dma_start(bias_rows[j:j + 1, :, :], bias_part[:, j, :, :]), part,
                                         counter=s_br)
            R["gate_bias_product"] = mm

        def gate_weights():
            mm = R["gate_bias_product"]
            for k in range(KD):
                gw = dve.do(lambda e, k=k: e.tensor_scalar(gate_f[:, k, :], gate_f[:, k, :], lnw_sb[:, k:k + 1], WS,
                                                           ALU.mult, ALU.mult), mm, lnw_in)
            hi = dve.do(lambda e: e.tensor_copy(gate_p[:, 0, :, :], gate_f[:, :, :]), gw)
            R["gate_w"] = dve.do(lambda e: e.tensor_tensor(gate_p[:, 1, :, :], gate_f[:, :, :], gate_p[:, 0, :, :],
                                                           ALU.subtract), hi)

        U, GATE = bank[6], bank[7]
        Z = {"f": xf_free[1], "parts": (), "T": (), "gate": ()}
        gate_ready = {}

        def z_norm(b):
            ready = rstd_ready[b * BT // SB]
            for i in range(BT):
                Z["zn"] = dve.do(lambda e, n=b * BT + i, i=i: e.tensor_scalar(
                    zn_f[:, i, :], x_sb[:, n, :], mean_var[:, n, 0:1], rstd2[:, 1, n:n + 1], ALU.subtract, ALU.mult),
                    ready, *Z["f"])

        def z_hi(b):
            Z["hi"] = act.do(lambda e: e.activation(zn_parts[:, :, 0, :], zn_f[:, :, :], ACT.Copy), Z["zn"], *Z["parts"])

        def z_lo(b):
            lo = dve.do(lambda e: e.tensor_tensor(zn_parts[:, :, 1, :], zn_f[:, :, :], zn_parts[:, :, 0, :],
                                                  ALU.subtract), Z["hi"], *Z["parts"])
            Z["f"], Z["made"] = (lo,), (Z["hi"], lo)

        def z_transpose(b, part):
            t, ev = transposed(lambda j: zn_parts[:, j % BT, part, (j // BT) * P:(j // BT + 1) * P], zT[:, part, :, :],
                               (Z["made"][part],), act if part == 0 else dve, *Z["T"])
            Z["parts"] = (t,)
            Z.setdefault("ev", []).append(ev)

        def z_input(b):
            ready, Z["ev"] = tuple(Z["ev"][-2:]), []
            Z["ready"] = ready
            steps = [(k, pz, pw) for k in range(KD) for pz, pw in SPLIT3]
            for j, (k, pz, pw) in enumerate(steps):
                R["u"] = pe.do(lambda e, j=j, k=k, pz=pz, pw=pw:
                               e.matmul(U[:, :], state_pad[:, pw, k, MID - b * N:MID - b * N + P], zT[:, pz, k, :],
                                        start=b == 0 and j == 0, stop=b == NB - 1 and j == len(steps) - 1),
                               *ready, R["state_w"], R["state_bias"], quiet=j < len(steps) - 1)

        def z_gate(b, half):
            for i2 in range(2):
                i = half * 2 + i2
                steps = [(k, pz, pw) for k in range(KD) for pz, pw in SPLIT3]
                for j, (k, pz, pw) in enumerate(steps):
                    pe.do(lambda e, i=i, i2=i2, j=j, k=k, pz=pz, pw=pw:
                          e.matmul(GATE[:, i2 * D:(i2 + 1) * D], zT[:, pz, k, i * P:(i + 1) * P], gate_p[:, pw, k, :],
                                   start=j == 0, stop=False), R["gate_w"], R["bias_0"], *Z["ready"], *Z["gate"],
                          quiet=True)
                gm = pe.do(lambda e, i2=i2: e.matmul(GATE[:, i2 * D:(i2 + 1) * D], ones_row3[:, :], bias_rows[:, 0, :],
                                                     start=False, stop=True), R["bias_rows"], ones_ready[1])
            n = b * BT + half * 2
            gs = act.do(lambda e: e.activation(mix_sb[:, n:n + 2, :].rearrange("p n d -> p (n d)"), GATE[:, :],
                                               ACT.Tanh, scale=0.5 * DESCALE), gm, R["weights"])
            Z["gate"], Z["T"] = (gs,), (gm,)
            gate_ready[n] = gate_ready[n + 1] = gs

        def u_done():
            R["u_sb"] = act.do(lambda e: e.activation(u_sb[:, :, :].rearrange("p c j -> p (c j)"), U[:, :], ACT.Identity,
                                                      bias=state_bias[:, 0:1], scale=DESCALE), R["u"], R["state_bias"])

        SP = [bank[6], bank[7]]
        scan = {"tanh": None, "n": 0, "start": None, "free": None}

        def scan_step(p, j):
            if scan["free"] is None:
                scan["free"] = [(R["u_sb"],), Z["gate"]]
            n = scan["n"]
            sp, first = SP[n % 2], p == 0 and j == 0
            a = pe.do(lambda e: e.matmul(sp[:, 0:C], ident_f[:, :], u_sb[:, :, j], start=True, stop=first), idf,
                      R["u_sb"], *scan["free"][n % 2])
            if not first:
                h = H[p][:, :, j - 1] if j else start[p - 1][:, :]
                a = pe.do(lambda e: e.matmul(sp[:, 0:C], rec_bd[:, :], h, start=False, stop=True), rec_in,
                          scan["tanh"] if j else scan["start"])
            t = act.do(lambda e: e.activation(H[p][:, :, j], sp[:, 0:C], ACT.Tanh), a)
            scan["tanh"], scan["n"], scan["free"][n % 2] = t, n + 1, (t,)

        def scan_shift(p):
            n = scan["n"]
            sp = SP[n % 2]
            m = pe.do(lambda e: e.matmul(sp[:, 0:1], shift_f[:, :], H[p][:, C - 1:C, L - 1], start=True, stop=True),
                      shift_ready, scan["tanh"], *scan["free"][n % 2])
            dve.do(lambda e: e.tensor_copy(start[p][:, 1:C], H[p][:, 0:C - 1, L - 1]), scan["tanh"])
            b = dve.do(lambda e: e.tensor_copy(start[p][:, 0:1], sp[:, 0:1]), m)
            scan["n"], scan["start"], scan["free"][n % 2] = n + 1, b, (b,)

        def scan_check():
            n = scan["n"]
            sp = SP[n % 2]
            d = dve.do(lambda e: e.tensor_tensor(differ[:, :], start[0][:, :], start[1][:, :], ALU.not_equal), scan["start"])
            d = dve.do(lambda e: e.tensor_reduce(differ_max[:, :], differ[:, :], AX.X, ALU.add), d)
            m = pe.do(lambda e: e.matmul(sp[0:1, 0:1], differ_max[:, :], ones_col[:, :], start=True, stop=True), d,
                      ones_ready[0], *scan["free"][n % 2])
            R["flag"] = dve.do(lambda e: e.tensor_copy(flag[:, :], sp[0:1, 0:1]), m)

        GU, HT, YP = [bank[2], bank[3]], bank[4], bank[5]
        s_xg = [sem(f"x_gathered{i}", 16) for i in range(XG_RING)]
        s_ys = [sem(f"y_scattered{i}", 16) for i in range(YS_RING)]
        M = {"gathered": {}, "xg_read": {}, "xT": {}, "gu": {}, "gu_free": {}, "h": {}, "ht_free": (), "yp_free": (),
             "scattered": {}, "down": {}, "ys": {}, "hf": {}, "htc": {}, "hT": {}}
        expert_value = {}

        def gather(n):
            free = (M["xg_read"][n - XG_RING],) if n >= XG_RING else (shared["last"], *xp_out)
            for j in range(min(2, USED - 2 * n)):
                M["gathered"][n] = pool.do(lambda e, j=j: e.indirect_dma_start(
                    out=x_ring[:, n % XG_RING, j, :], out_offset=None, in_=x_parts_dram,
                    in_offset=bass.IndirectOffsetOnAxis(ap=token_of[:, 2 * n + j:2 * n + j + 1], axis=0)),
                    R["tokens"], *free, counter=s_xg[n % XG_RING])

        def scatter(n):
            for j in range(min(2, USED - 2 * n)):
                M["scattered"][n] = pool.do(lambda e, j=j: e.indirect_dma_start(
                    out=y_dram, out_offset=bass.IndirectOffsetOnAxis(ap=row_of[:, 2 * n + j:2 * n + j + 1], axis=0),
                    in_=y_ring[:, n % YS_RING, j, :], in_offset=None), R["rows"], M["ys"][n],
                    counter=s_ys[n % YS_RING])

        VL = 8

        def load_experts(b0):
            def make(e):
                loads, values = nc.values_load_multi_w_load_instructions(
                    expert_of[0:1, b0:b0 + VL], engines=[e.engine], min_val=0, max_val=E - 1,
                    skip_runtime_bounds_check_because="a count of at most E experts, clamped to E - 1 on the chip")
                for i, v in enumerate(values):
                    expert_value[b0 + i] = v
                return loads[-1]
            pe.do(make, R["experts"], quiet=True)

        def pair_x(n):
            s = n % 2
            free = (M["gu"][n - 2],) if n >= 2 else (shared["last"],)
            t, M["xT"][n] = transposed(lambda j: x_ring[:, n % XG_RING, j // 4, (j % 4) * P:(j % 4 + 1) * P],
                                       xg_T[:, s, :], (M["gathered"][n],), dve, *free)
            M["xg_read"][n] = t

        def pair_up(n):
            gu = GU[n % 2]
            for j in range(2):
                b = 2 * n + j
                if b % VL == 0:
                    load_experts(b)
                steps = [(k, px, pw) for k in range(KD) for px, pw in SPLIT3]
                for i, (k, px, pw) in enumerate(steps):
                    M["gu"][n] = pe.do(lambda e, b=b, j=j, i=i, k=k, px=px, pw=pw: e.matmul(
                        gu[:, j * 2 * F:(j + 1) * 2 * F],
                        xg_T[:, n % 2, ((j * 2 + px) * KD + k) * P:((j * 2 + px) * KD + k + 1) * P],
                        w_all[:, bass.ds(expert_value[b], 1), pw * WG + k * 2 * F:pw * WG + (k + 1) * 2 * F],
                        start=i == 0, stop=i == len(steps) - 1), M["xT"][n], *all_w,
                        *M["gu_free"].get(n - 2, gu_first), quiet=i < len(steps) - 1)
            gv = gu[:, :].rearrange("p (b f) -> p b f", b=2)
            sg = act.do(lambda e: e.activation(silu_sb[:, n % 2, :, :], gv[:, :, 0:F], ACT.Silu, scale=DESCALE),
                        M["gu"][n], *M["hf"].get(n - 2, ()))
            hf = dve.do(lambda e: e.scalar_tensor_tensor(out=h_sb[:, n % 2, :, :], in0=gv[:, :, F:2 * F], scalar=DESCALE,
                                                         in1=silu_sb[:, n % 2, :, :], op0=ALU.mult, op1=ALU.mult), sg,
                        *M["hf"].get(n - 2, ()))
            M["gu_free"][n] = (hf,)

        def pair_split(n):
            hf, = M["gu_free"][n]
            hh = act.do(lambda e: e.activation(h_parts[:, n % 2, :, 0, :], h_sb[:, n % 2, :, :], ACT.Copy), hf,
                        *M["htc"].get(n - 2, ()))
            hl = dve.do(lambda e: e.tensor_tensor(h_parts[:, n % 2, :, 1, :], h_sb[:, n % 2, :, :],
                                                  h_parts[:, n % 2, :, 0, :], ALU.subtract), hh)
            M["h"][n], M["hf"][n] = (hh, hl), (hl,)

        def pair_h(n):
            tb = HT[:, :].bitcast(f16)
            for q in range(4):
                t = pe.do(lambda e, q=q: e.transpose(tb[:, q * P:(q + 1) * P], h_parts[:, n % 2, q // 2, q % 2, :],
                                                     ident_h[:, :]), *M["h"][n], *M["ht_free"], quiet=q < 3)
            M["htc"][n] = (t,)
            c = dve.do(lambda e: e.tensor_copy(hT_sb[:, n % 2, :, :, :].rearrange("p b i f -> p (b i f)"), tb[:, 0:4 * P]),
                       t, *((M["down"][n - 2],) if n >= 2 else ()))
            M["ht_free"], M["hT"][n] = (c,), c

        def pair_down(n):
            for j in range(2):
                for i, (ph, pw) in enumerate(SPLIT3):
                    m = pe.do(lambda e, b=2 * n + j, j=j, i=i, ph=ph, pw=pw: e.matmul(
                        YP[:, j * D:(j + 1) * D], hT_sb[:, n % 2, j, ph, :],
                        w_all[:, bass.ds(expert_value[b], 1), 2 * WG + pw * W2:2 * WG + (pw + 1) * W2],
                        start=i == 0, stop=i == 2), M["hT"][n], *M["yp_free"], quiet=not (i == 2 and j == 1))
            M["down"][n] = m
            r = n % YS_RING
            free = (M["scattered"][n - YS_RING],) if n >= YS_RING else ()
            y = act.do(lambda e: e.activation(y_ring[:, r, :, :].rearrange("p b d -> p (b d)"), YP[:, :], ACT.Copy),
                       m, *free)
            M["yp_free"], M["ys"][n] = (y,), y

        fb = {k: ctx.enter_context(nc.semaphore(f"fb_{k}")) for k in ("sum", "state", "next", "copied", "end_act", "end_dve")}

        def differs(eng):
            flag_ready = R["flag"]
            eng.wait_ge(flag_ready[0].handle, flag_ready[1])
            return eng.value_load(flag[0:1, 0:1], min_val=0, max_val=P * C)

        def take(eng, s):
            eng.wait_ge(s, 1)
            eng.sem_inc(s, -1)

        PASSES = T // SEQS // L - 1

        def fallback_pe(eng):
            v = differs(eng)
            with eng.If(v != 0):
                with eng.Fori(0, PASSES):
                    for j in range(L):
                        eng.matmul(SP[0][:, 0:C], ident_f[:, :], u_sb[:, :, j], start=True, stop=False)
                        h = H[1][:, :, j - 1] if j else start[1][:, :]
                        eng.matmul(SP[0][:, 0:C], rec_bd[:, :], h, start=False, stop=True).then_inc(fb["sum"], 1)
                        take(eng, fb["state"])
                    eng.matmul(SP[1][:, 0:1], shift_f[:, :], H[1][:, C - 1:C, L - 1], start=True, stop=True)\
                        .then_inc(fb["next"], 1)
                    take(eng, fb["copied"])
                eng.sem_inc(fb["end_act"], 1)
                eng.sem_inc(fb["end_dve"], 1)

        def fallback_act(eng):
            v = differs(eng)
            with eng.If(v != 0):
                with eng.Fori(0, PASSES):
                    for j in range(L):
                        take(eng, fb["sum"])
                        eng.activation(H[1][:, :, j], SP[0][:, 0:C], ACT.Tanh).then_inc(fb["state"], 1)
                take(eng, fb["end_act"])

        def fallback_dve(eng):
            v = differs(eng)
            with eng.If(v != 0):
                with eng.Fori(0, PASSES):
                    take(eng, fb["next"])
                    eng.tensor_copy(start[1][:, 1:C], H[1][:, 0:C - 1, L - 1])
                    eng.tensor_copy(start[1][:, 0:1], SP[1][:, 0:1]).then_inc(fb["copied"], 1)
                take(eng, fb["end_dve"])

        room = [stages, zT[:, :, :, :].rearrange("p i k t -> p (i k t)").bitcast(f32),
                zn_parts[:, :, :, :].rearrange("p b i d -> p (b i d)").bitcast(f32)]
        room = [v.rearrange("p (n d) -> p n d", d=D) for v in room]
        shared_early = [(v, i) for v in room for i in range(v.shape[1])]
        EARLY = len(shared_early)

        def shared_back():
            s_back, first = sem("shared_back", 16), 0
            for v in room:
                tiles = slice(first, first + v.shape[1])
                R["early"] = sync.do(lambda e, v=v, tiles=tiles: e.dma_start(v, ysh_view[:, tiles, :]),
                                     *shared["y_free"][0], *shared["y_free"][1], R["gate_w"], R["state_w"],
                                     R["state_bias"], R["bias_rows"], *Z["T"], *Z["parts"], *Z["f"], counter=s_back)
                first += v.shape[1]

        def general_recurrence():
            for q, steps in ((pe, fallback_pe), (act, fallback_act), (dve, fallback_dve)):
                q.do(steps, quiet=True)

        O = {"free": [(), ()]}
        Hv = [H_p[:, i, :, :].rearrange("p c j -> p (c j)") for i in range(2)]

        def out_weights():
            outw_in = sync.do(lambda e: e.dma_start(zn_f[:, 1, :], out_wt), *Z["f"], counter=sem("outw_in", 16))
            hi = dve.do(lambda e: e.tensor_scalar(outw_c[:, 0, :], zn_f[:, 1, :], WS, None, ALU.mult), outw_in)
            lo = dve.do(lambda e: e.scalar_tensor_tensor(out=outw_c[:, 1, :], in0=zn_f[:, 1, :], scalar=WS,
                                                         in1=outw_c[:, 0, :], op0=ALU.mult, op1=ALU.subtract), hi)
            s_ow = sem("outw_placed", 16)
            for g in range(G):
                O["w"] = sync.do(lambda e, g=g: e.dma_start(outw_p[g * N:(g + 1) * N, :, g, :],
                                                            outw_c[g * N:(g + 1) * N, :, :]), lo, O["zero"], counter=s_ow)

        def out_padding():
            O["zero"] = dve.do(lambda e: e.memset(outw_p[:, :, :, :], 0.0), shared["last"])

        def state_parts():
            O["rstd"] = dve.do(lambda e: e.tensor_scalar(xn_scale[:, :], rstd2[:, 0, :], 1.0 / XS, None, ALU.mult))
            O["bias"] = dve.do(lambda e: e.scalar_tensor_tensor(out=xn_bias[:, :], in0=mean_var[:, :, 0], scalar=-1.0,
                                                                in1=xn_scale[:, :], op0=ALU.mult, op1=ALU.mult), O["rstd"])
            hh = act.do(lambda e: e.activation(H_p[:, 0, :, :], H[1][:, :, :], ACT.Copy, scale=XS), R["flag"])
            O["h"] = (hh, dve.do(lambda e: e.scalar_tensor_tensor(out=H_p[:, 1, :, :], in0=H[1][:, :, :], scalar=XS,
                                                                  in1=H_p[:, 0, :, :], op0=ALU.mult, op1=ALU.subtract), hh))

        def out_mix(n):
            ob, g, i = SP[n % 2], n // BT, n % BT
            for j, (ph, pw) in enumerate(SPLIT3):
                pe.do(lambda e, j=j, ph=ph, pw=pw, ob=ob, g=g, i=i:
                      e.matmul(ob[:, 0:D], Hv[ph][:, i * P:(i + 1) * P], outw_p[:, pw, g, :], start=j == 0, stop=False),
                      *O["h"], O["w"], *O["free"][n % 2], quiet=True)
            om = pe.do(lambda e, ob=ob: e.matmul(ob[:, 0:D], ones_row3[:, :], bias_rows[:, 1, :], start=False, stop=True),
                       R["bias_rows"])
            q = act.do(lambda e: e.activation(xn_f[:, n % BT, :], x_sb[:, n, :], ACT.Identity, bias=xn_bias[:, n:n + 1],
                                              scale=xn_scale[:, n:n + 1]),
                       *shared["y_free"][0], *shared["y_free"][1], O["bias"], *O.get(("q", n - BT), ()))
            a = dve.do(lambda e: e.scalar_tensor_tensor(out=mix_sb[:, n, :], in0=mix_sb[:, n, :], scalar=1.0,
                                                        in1=ob[:, 0:D], op0=ALU.add, op1=ALU.mult), om, gate_ready[n])
            O["free"][n % 2] = (a,)
            O["mix", n] = dve.do(lambda e: e.scalar_tensor_tensor(
                out=mix_sb[:, n, :], in0=mix_sb[:, n, :], scalar=0.5 * DESCALE, in1=xn_f[:, n % BT, :], op0=ALU.mult,
                op1=ALU.add), a, q)
            O["q", n] = (O["mix", n],)

        route_blocks()
        shared_down(0)
        shared_up(1)
        route_slots()
        shared_hidden(1)
        shared_down(1)
        ahead = 2
        for n in range(NT):
            table_tile(n)
            if n:
                table_product(n - 1)
            b = ahead + n // 5
            if n % 5 == 0 and b < NB:
                shared_up(b)
            if n % 5 == 3 and b < NB:
                shared_hidden(b)
            if n % 5 == 1 and ahead < b <= NB:
                shared_down(b - 1)
            if n % 3 == 0 and NB + n // 3 <= E:
                split_weights(NB + n // 3)
        table_product(NT - 1)
        finish_table()
        all_w = w_ready[E - 1]
        gu_first = (R["sc"], R["slot_e"])
        M["yp_free"], M["ht_free"] = shared["up_free"], shared["up_free"]
        tp["free"] = list(shared["free"])

        SLOTS = 3
        load_small()
        side = [None, (pick_weights, 0), None, (pick_weights, 1), None, (pick_weights, 2), None, (pick_weights, 3), None,
                (state_weights,), None, (state_bias_sum,), (z_norm, 0), None, (z_hi, 0), (bias_weights,), None,
                (z_lo, 0), (route_weights,), None, (gate_weights,), None, (z_transpose, 0, 0), (z_transpose, 0, 1), None]
        for b in range(NB):
            more = b + 1 < NB
            side += [(z_input, b), (z_norm, b + 1) if more else None, None, (z_gate, b, 0),
                     (z_hi, b + 1) if more else None, (z_lo, b + 1) if more else None, (z_gate, b, 1), None]
            side += [(z_transpose, b + 1, 0), (z_transpose, b + 1, 1), None] if more else []
        side += [(u_done,), (shared_back,), (out_padding,)]
        for p in range(2):
            side += [step for j in range(0, L, 2) for step in ((scan_step, p, j), (scan_step, p, j + 1), None)]
            side += [(scan_shift, p)]
        side += [(out_weights,), (scan_check,), None, None, None, (general_recurrence,), (state_parts,), None, None]
        side += [(out_mix, n) for n in range(NT)]
        assert len(side) <= SLOTS * NPAIR

        def beside(slot):
            if slot < len(side) and side[slot] is not None:
                step, *args = side[slot]
                step(*args)

        AHEAD, LAG = XG_RING - 2, 4
        for n in range(AHEAD):
            gather(n)
        pair_x(0)
        pair_x(1)
        pair_up(0)
        pair_split(0)
        for n in range(NPAIR + 1):
            if n + AHEAD < NPAIR:
                gather(n + AHEAD)
            if n >= LAG:
                scatter(n - LAG)
            if n + 2 < NPAIR:
                pair_x(n + 2)
            beside(SLOTS * n)
            if n + 1 < NPAIR:
                pair_up(n + 1)
                pair_split(n + 1)
            beside(SLOTS * n + 1)
            if n < NPAIR:
                pair_h(n)
            beside(SLOTS * n + 2)
            if n >= 1:
                pair_down(n - 1)
        for n in range(NPAIR + 1 - LAG, NPAIR):
            scatter(n)
        all_scattered = [M["scattered"][n] for n in range(NPAIR - YS_RING, NPAIR)]

        s_yin = [sem(f"y_in{i}", 16) for i in range(FIN_RING)]
        s_out = [sem(f"out_stored{i}", 16) for i in range(FIN_RING)]
        y_view = y_dram[0:T * TOPK, :].rearrange("(n p k) d -> p n k d", p=P, k=TOPK)
        o_view = out.rearrange("(n p) d -> p n d", p=P)
        last_pe = M["down"][NPAIR - 1]
        stored, y_in, product = {}, {}, {}

        def load_results(i):
            r, tiles = i % FIN_RING, slice(i * FT, (i + 1) * FT)
            free = (product[i - FIN_RING],) if i >= FIN_RING else (last_pe,)
            if i * FT >= EARLY:
                sync.do(lambda e: e.dma_start(fin_sum[:, r, :, :], ysh_view[:, tiles, :]), *shared["y_free"][0],
                        *shared["y_free"][1], *free, counter=s_yin[r])
            y_in[i] = sync.do(lambda e: e.dma_start(fin_y[:, r, :, :, :], y_view[:, tiles, :, :]), *all_scattered, *free,
                              counter=s_yin[r])

        def combine(i):
            r, tiles = i % FIN_RING, slice(i * FT, (i + 1) * FT)
            c = [y_in[i]] * FT
            for k in range(TOPK):
                for j in range(FT):
                    n, acc = i * FT + j, fin_sum[:, r, j, :]
                    so_far = acc
                    if n < EARLY and k == 0:
                        v, at_tile = shared_early[n]
                        so_far = v[:, at_tile, :]
                    free = (product[i - FIN_RING],) if i >= FIN_RING else (last_pe,)
                    c[j] = dve.do(lambda e, n=n, j=j, k=k, acc=acc, so_far=so_far: e.scalar_tensor_tensor(
                        out=acc, in0=fin_y[:, r, j, k, :], scalar=topk_w[:, n, k:k + 1], in1=so_far, op0=ALU.mult,
                        op1=ALU.add), c[j], R["weights"], R["early"], *free)
            sg = act.do(lambda e: e.activation(fin_sum[:, r, :, :], fin_sum[:, r, :, :], ACT.Silu), *c)
            product[i] = pool.do(lambda e: e.tensor_tensor(mix_sb[:, tiles, :], fin_sum[:, r, :, :], mix_sb[:, tiles, :],
                                                           ALU.mult), sg, *(O["mix", i * FT + j] for j in range(FT)))

        def store(i):
            tiles = slice(i * FT, (i + 1) * FT)
            m = pool.do(lambda e: e.tensor_tensor(mix_sb[:, tiles, :], mix_sb[:, tiles, :], x_sb[:, tiles, :], ALU.add),
                        product[i])
            stored[i] = act.do(lambda e: e.dma_start(o_view[:, tiles, :], mix_sb[:, tiles, :]), m,
                               counter=s_out[i % FIN_RING])

        NF = NT // FT
        for i in range(FIN_RING - 1):
            load_results(i)
        for i in range(NF):
            combine(i)
            if i:
                store(i - 1)
            if i + FIN_RING - 1 < NF:
                load_results(i + FIN_RING - 1)
        store(NF - 1)
        for i in range(NF - FIN_RING, NF):
            sync.do(lambda e: e.nop(), stored[i], quiet=True)

        block = ctx.enter_context(nc.Block())

        @block.tensor
        def _(eng):
            pe.emit(eng)

        @block.scalar
        def _(eng):
            act.emit(eng)

        @block.vector
        def _(eng):
            dve.emit(eng)

        @block.gpsimd
        def _(eng):
            pool.emit(eng)

        @block.sync
        def _(eng):
            sync.emit(eng)


def kernel(**inputs):
    import concourse.bacc as bacc
    from concourse.bass_utils import run_bass_kernel_spmd

    a = {k: np.asarray(v) for k, v in inputs.items()}
    P = 128
    B, S, D = a["L0_attn_x"].shape

    def on_partitions(w):
        return w.reshape(w.shape[0], D // P, P).transpose(2, 1, 0)

    w13 = np.concatenate([a["L0_ffn_w13"], a["L0_ffn_w13_s"][None]])
    w2 = np.concatenate([a["L0_ffn_w2"], a["L0_ffn_w2_s"][None]])
    n_e, gu, _ = w13.shape
    n = a["L0_attn_A"].shape[0]
    arrays = {
        "x": a["L0_attn_x"].reshape(B * S, D),
        "w13t": w13.reshape(n_e, gu, D // P, P).transpose(3, 0, 2, 1).reshape(P, n_e, (D // P) * gu),
        "w2t": w2.transpose(2, 0, 1),
        "router_wt": on_partitions(a["L0_ffn_gate_w"]),
        "router_b": a["L0_ffn_gate_b"][None],
        "gate_wt": on_partitions(a["L0_attn_Wg"]),
        "gate_b_row": a["L0_attn_bg"][None],
        "state_wt": on_partitions(a["L0_attn_Ws"]),
        "input_wt": on_partitions(a["L0_attn_Wi"]),
        "state_b": np.tile(a["L0_attn_bs"], P // n)[:, None],
        "input_b": np.tile(a["L0_attn_bi"], P // n)[:, None],
        "rec_at": a["L0_attn_A"].T,
        "out_wt": np.tile(a["L0_attn_Wo"].T, (P // n, 1)),
        "out_b_row": a["L0_attn_bo"][None],
        "ln_w": a["L0_attn_ln_w"].reshape(D // P, P).T,
        "ln_b": a["L0_attn_ln_b"].reshape(D // P, P).T,
    }
    arrays = {f"in_{k}": np.ascontiguousarray(v) for k, v in arrays.items()}
    nc = bacc.Bacc("TRN2", target_bir_lowering=False, num_devices=1)
    args = [nc.dram_tensor(k, v.shape, mybir.dt.from_np(v.dtype), kind="ExternalInput").ap() for k, v in arrays.items()]
    out = nc.dram_tensor("out", (B * S, D), mybir.dt.float32, kind="ExternalOutput").ap()
    tokens, topk = B * S, 4
    x_parts = nc.dram_tensor("x_parts", (tokens, 2 * D), mybir.dt.float16, kind="Internal").ap()
    routed_y = nc.dram_tensor("routed_y", (tokens * topk + (tokens * topk // P + a["L0_ffn_gate_w"].shape[0]) * P, D), mybir.dt.float32, kind="Internal").ap()
    shared_y = nc.dram_tensor("shared_y", (tokens, D), mybir.dt.float32, kind="Internal").ap()
    recurrent_gated_moe(nc, *args, out, x_parts, routed_y, shared_y)
    r = run_bass_kernel_spmd(nc, [arrays], core_ids=[0])
    return r.results[0]["out"].reshape(B, S, D)
```
